# Optimizing a Trainium2 kernel written in Bass

```python
import numpy as np
import jax
import jax.numpy as jnp

def _softmax(x, axis=-1):
    return jax.nn.softmax(x, axis=axis)

def _gelu(x):
    return jax.nn.gelu(x, approximate=True)

def _silu(x):
    return jax.nn.silu(x)

def _sigmoid(x):
    return jax.nn.sigmoid(x)

def _layernorm(x, axis=-1, eps=1e-05):
    m = jnp.mean(x, axis=axis, keepdims=True)
    v = jnp.var(x, axis=axis, keepdims=True)
    return (x - m) / jnp.sqrt(v + eps)

def _scatter_add(tgt, idx, src, axis=0):
    return tgt.at[idx].add(src)

def _segment_sum(src, seg, n):
    return jax.ops.segment_sum(src, seg, n)
kernel_name = 'mk_dlrm_tower_d1_rec_r8_a5f555'

def setup_inputs(seed: int=0):
    np.random.seed(seed)
    _w = jnp.asarray

    def _rec_inputs():
        import jax
        import jax.numpy as jnp
        _tk = jax.random.key(seed)
        dense_ctx = jax.random.normal(jax.random.fold_in(_tk, 190), (2048, 16), jnp.float32)
        ids = jnp.stack([jax.random.randint(jax.random.fold_in(_tk, 200 + f), (2048,), 0, v, jnp.int32) for f, v in enumerate([1000, 125000, 1250, 12500, 12500, 1250, 1000, 1000, 12500, 12500, 125000, 12500, 125000, 12500, 1250, 1000, 1250, 1250, 12500, 1000, 12500, 1000, 1000, 1000, 1000, 1000, 1250, 1250, 1000, 1000, 1000, 1000])], axis=1)
        tbl_0 = 0.05 * jax.random.normal(jax.random.fold_in(_tk, 500 + 0), (1000, 64), jnp.float32)
        tbl_1 = 0.05 * jax.random.normal(jax.random.fold_in(_tk, 500 + 1), (125000, 64), jnp.float32)
        tbl_2 = 0.05 * jax.random.normal(jax.random.fold_in(_tk, 500 + 2), (1250, 64), jnp.float32)
        tbl_3 = 0.05 * jax.random.normal(jax.random.fold_in(_tk, 500 + 3), (12500, 64), jnp.float32)
        tbl_4 = 0.05 * jax.random.normal(jax.random.fold_in(_tk, 500 + 4), (12500, 64), jnp.float32)
        tbl_5 = 0.05 * jax.random.normal(jax.random.fold_in(_tk, 500 + 5), (1250, 64), jnp.float32)
        tbl_6 = 0.05 * jax.random.normal(jax.random.fold_in(_tk, 500 + 6), (1000, 64), jnp.float32)
        tbl_7 = 0.05 * jax.random.normal(jax.random.fold_in(_tk, 500 + 7), (1000, 64), jnp.float32)
        tbl_8 = 0.05 * jax.random.normal(jax.random.fold_in(_tk, 500 + 8), (12500, 64), jnp.float32)
        tbl_9 = 0.05 * jax.random.normal(jax.random.fold_in(_tk, 500 + 9), (12500, 64), jnp.float32)
        tbl_10 = 0.05 * jax.random.normal(jax.random.fold_in(_tk, 500 + 10), (125000, 64), jnp.float32)
        tbl_11 = 0.05 * jax.random.normal(jax.random.fold_in(_tk, 500 + 11), (12500, 64), jnp.float32)
        tbl_12 = 0.05 * jax.random.normal(jax.random.fold_in(_tk, 500 + 12), (125000, 64), jnp.float32)
        tbl_13 = 0.05 * jax.random.normal(jax.random.fold_in(_tk, 500 + 13), (12500, 64), jnp.float32)
        tbl_14 = 0.05 * jax.random.normal(jax.random.fold_in(_tk, 500 + 14), (1250, 64), jnp.float32)
        tbl_15 = 0.05 * jax.random.normal(jax.random.fold_in(_tk, 500 + 15), (1000, 64), jnp.float32)
        tbl_16 = 0.05 * jax.random.normal(jax.random.fold_in(_tk, 500 + 16), (1250, 64), jnp.float32)
        tbl_17 = 0.05 * jax.random.normal(jax.random.fold_in(_tk, 500 + 17), (1250, 64), jnp.float32)
        tbl_18 = 0.05 * jax.random.normal(jax.random.fold_in(_tk, 500 + 18), (12500, 64), jnp.float32)
        tbl_19 = 0.05 * jax.random.normal(jax.random.fold_in(_tk, 500 + 19), (1000, 64), jnp.float32)
        tbl_20 = 0.05 * jax.random.normal(jax.random.fold_in(_tk, 500 + 20), (12500, 64), jnp.float32)
        tbl_21 = 0.05 * jax.random.normal(jax.random.fold_in(_tk, 500 + 21), (1000, 64), jnp.float32)
        tbl_22 = 0.05 * jax.random.normal(jax.random.fold_in(_tk, 500 + 22), (1000, 64), jnp.float32)
        tbl_23 = 0.05 * jax.random.normal(jax.random.fold_in(_tk, 500 + 23), (1000, 64), jnp.float32)
        tbl_24 = 0.05 * jax.random.normal(jax.random.fold_in(_tk, 500 + 24), (1000, 64), jnp.float32)
        tbl_25 = 0.05 * jax.random.normal(jax.random.fold_in(_tk, 500 + 25), (1000, 64), jnp.float32)
        tbl_26 = 0.05 * jax.random.normal(jax.random.fold_in(_tk, 500 + 26), (1250, 64), jnp.float32)
        tbl_27 = 0.05 * jax.random.normal(jax.random.fold_in(_tk, 500 + 27), (1250, 64), jnp.float32)
        tbl_28 = 0.05 * jax.random.normal(jax.random.fold_in(_tk, 500 + 28), (1000, 64), jnp.float32)
        tbl_29 = 0.05 * jax.random.normal(jax.random.fold_in(_tk, 500 + 29), (1000, 64), jnp.float32)
        tbl_30 = 0.05 * jax.random.normal(jax.random.fold_in(_tk, 500 + 30), (1000, 64), jnp.float32)
        tbl_31 = 0.05 * jax.random.normal(jax.random.fold_in(_tk, 500 + 31), (1000, 64), jnp.float32)
        _rk = jax.random.fold_in(_tk, 7)
        W_top1 = 0.0428746 * jax.random.normal(jax.random.fold_in(_tk, 801), (544, 512), jnp.float32)
        W_top2 = 0.0441942 * jax.random.normal(jax.random.fold_in(_tk, 802), (512, 256), jnp.float32)
        W_top3 = 0.0625 * jax.random.normal(jax.random.fold_in(_tk, 803), (256, 1), jnp.float32)
        b_top1 = jnp.zeros((512,), jnp.float32)
        b_top2 = jnp.zeros((256,), jnp.float32)
        return (dense_ctx, ids, tbl_0, tbl_1, tbl_2, tbl_3, tbl_4, tbl_5, tbl_6, tbl_7, tbl_8, tbl_9, tbl_10, tbl_11, tbl_12, tbl_13, tbl_14, tbl_15, tbl_16, tbl_17, tbl_18, tbl_19, tbl_20, tbl_21, tbl_22, tbl_23, tbl_24, tbl_25, tbl_26, tbl_27, tbl_28, tbl_29, tbl_30, tbl_31, W_top1, b_top1, W_top2, b_top2, W_top3)
    dense_ctx, ids, tbl_0, tbl_1, tbl_2, tbl_3, tbl_4, tbl_5, tbl_6, tbl_7, tbl_8, tbl_9, tbl_10, tbl_11, tbl_12, tbl_13, tbl_14, tbl_15, tbl_16, tbl_17, tbl_18, tbl_19, tbl_20, tbl_21, tbl_22, tbl_23, tbl_24, tbl_25, tbl_26, tbl_27, tbl_28, tbl_29, tbl_30, tbl_31, W_top1, b_top1, W_top2, b_top2, W_top3 = _rec_inputs()

    def _L0_rec_setup():
        import jax, jax.numpy as jnp
        import numpy as np
        B, F, D = (512, 32, 64)
        II, JJ = np.triu_indices(F, k=1)
        P = II.shape[0]
        key = jax.random.key(seed)
        kx, kk = jax.random.split(key)
        x = jax.random.normal(kx, (B, F, D), dtype=jnp.float32)
        kernels = jax.random.normal(kk, (P, D, D), dtype=jnp.float32) * 0.001
        return {'x': x, 'kernels': kernels}
    _L0_rec_all = _L0_rec_setup()
    _L0_rec_in = {k: v for k, v in _L0_rec_all.items() if k in ('kernels',)}
    del _L0_rec_all
    return {'dense_ctx': dense_ctx, 'ids': ids, 'tbl_0': tbl_0, 'tbl_1': tbl_1, 'tbl_2': tbl_2, 'tbl_3': tbl_3, 'tbl_4': tbl_4, 'tbl_5': tbl_5, 'tbl_6': tbl_6, 'tbl_7': tbl_7, 'tbl_8': tbl_8, 'tbl_9': tbl_9, 'tbl_10': tbl_10, 'tbl_11': tbl_11, 'tbl_12': tbl_12, 'tbl_13': tbl_13, 'tbl_14': tbl_14, 'tbl_15': tbl_15, 'tbl_16': tbl_16, 'tbl_17': tbl_17, 'tbl_18': tbl_18, 'tbl_19': tbl_19, 'tbl_20': tbl_20, 'tbl_21': tbl_21, 'tbl_22': tbl_22, 'tbl_23': tbl_23, 'tbl_24': tbl_24, 'tbl_25': tbl_25, 'tbl_26': tbl_26, 'tbl_27': tbl_27, 'tbl_28': tbl_28, 'tbl_29': tbl_29, 'tbl_30': tbl_30, 'tbl_31': tbl_31, 'W_top1': W_top1, 'b_top1': b_top1, 'W_top2': W_top2, 'b_top2': b_top2, 'W_top3': W_top3, 'L0_rec_kernels': _L0_rec_in['kernels']}

def reference(dense_ctx, ids, tbl_0, tbl_1, tbl_2, tbl_3, tbl_4, tbl_5, tbl_6, tbl_7, tbl_8, tbl_9, tbl_10, tbl_11, tbl_12, tbl_13, tbl_14, tbl_15, tbl_16, tbl_17, tbl_18, tbl_19, tbl_20, tbl_21, tbl_22, tbl_23, tbl_24, tbl_25, tbl_26, tbl_27, tbl_28, tbl_29, tbl_30, tbl_31, W_top1, b_top1, W_top2, b_top2, W_top3, L0_rec_kernels):
    import jax
    import jax.numpy as jnp

    def _L0_rec_ref(x, kernels):
        import jax, jax.numpy as jnp
        import numpy as np
        B, F, D = (512, 32, 64)
        II, JJ = np.triu_indices(F, k=1)
        P = II.shape[0]
        z = jnp.sum(x, axis=-1)
        xi = x[:, II, :]
        xj = x[:, JJ, :]
        outer = jnp.einsum('bpd,pde,bpe->bp', xi, kernels, xj)
        return jnp.concatenate([z, outer], axis=1)
    e = jnp.stack([tbl_0[ids[:, 0]], tbl_1[ids[:, 1]], tbl_2[ids[:, 2]], tbl_3[ids[:, 3]], tbl_4[ids[:, 4]], tbl_5[ids[:, 5]], tbl_6[ids[:, 6]], tbl_7[ids[:, 7]], tbl_8[ids[:, 8]], tbl_9[ids[:, 9]], tbl_10[ids[:, 10]], tbl_11[ids[:, 11]], tbl_12[ids[:, 12]], tbl_13[ids[:, 13]], tbl_14[ids[:, 14]], tbl_15[ids[:, 15]], tbl_16[ids[:, 16]], tbl_17[ids[:, 17]], tbl_18[ids[:, 18]], tbl_19[ids[:, 19]], tbl_20[ids[:, 20]], tbl_21[ids[:, 21]], tbl_22[ids[:, 22]], tbl_23[ids[:, 23]], tbl_24[ids[:, 24]], tbl_25[ids[:, 25]], tbl_26[ids[:, 26]], tbl_27[ids[:, 27]], tbl_28[ids[:, 28]], tbl_29[ids[:, 29]], tbl_30[ids[:, 30]], tbl_31[ids[:, 31]]], axis=1)
    z = _L0_rec_ref(e, L0_rec_kernels)
    z = z.reshape(z.shape[0], -1)
    h = jnp.concatenate([z, dense_ctx], axis=1)
    h = jnp.maximum(h @ W_top1 + b_top1, 0.0)
    h = jnp.maximum(h @ W_top2 + b_top2, 0.0)
    y = h @ W_top3
    return y

_drawn_inputs = setup_inputs


def setup_inputs(seed=0):
    import zlib

    import numpy as np

    out = dict(_drawn_inputs(seed))
    spreads = {'b_top1': (0.0, 0.1), 'b_top2': (0.0, 0.1)}
    factors = {'L0_rec_kernels': 64.0}
    for name, (base, spread) in spreads.items():
        noise = np.random.default_rng([zlib.crc32(name.encode()), seed]).standard_normal(out[name].shape)
        drawn = base * np.exp(spread * noise) if base else spread * noise
        out[name] = jnp.asarray(drawn.astype(out[name].dtype))
    for name, factor in factors.items():
        out[name] = (out[name] * factor).astype(out[name].dtype)
    return out
```

```python
import concourse.bass as bass
from concourse import mybir
from contextlib import ExitStack

P = 128
BATCH, FIELDS, DIM = 2048, 32, 64
DENSE = 16
N1, N2 = 512, 256
COUPLES = FIELDS // 2
TILE = 512
TILES = BATCH // TILE
ROWSETS = TILE // P
GATHER_SLOTS = 4
Y_SLOTS = 3
PROD_SLOTS = 4
QUADS = 4
UNITS_PER_CHUNK = 64
RAW_CHUNKS = 16
RAW_SLOTS = 4


def interaction_units():
    units = []
    for i in range(FIELDS - 2, -1, -1):
        couples = list(range((i + 1) // 2 if i % 2 else i // 2, COUPLES))
        if i % 2 == 0:
            couples.reverse()
        units += [(i, m) for m in couples]
    for j in range(0, len(units), 2):
        if units[j][1] > units[j + 1][1]:
            units[j], units[j + 1] = units[j + 1], units[j]
    return units


def single(unit):
    return unit[0] == 2 * unit[1]


UNITS = interaction_units()
PAIRS = FIELDS * (FIELDS - 1) // 2
BLOCKS = 2 * len(UNITS)
CHUNKS = len(UNITS) // UNITS_PER_CHUNK
RAW_BLOCKS = BLOCKS // RAW_CHUNKS


def slot_ops():
    ops = [("x", COUPLES - 1), ("x", COUPLES - 2)]
    due = {}
    for j in range(len(UNITS) // 2):
        for u in (2 * j, 2 * j + 1):
            i = UNITS[u][0]
            if i % 2 == 0 and i >= 4:
                due[(i - 4) // 2] = j
    for j in range(len(UNITS) // 2):
        ops.append(("u", j))
        ops += [("x", m) for m in sorted(due, reverse=True) if due[m] == j]
    return ops


OPS = slot_ops()
N_OPS = len(OPS)
N_PROD = len(UNITS) // 2
N_GROUPS = N_PROD // 2
GROUPS_PER_CHUNK = UNITS_PER_CHUNK // QUADS
assert N_OPS % Y_SLOTS == 0 and N_PROD % PROD_SLOTS == 0


assert len(UNITS) - COUPLES + len(UNITS) == PAIRS


def op_at(kind, what):
    return OPS.index((kind, what))


def z_row(u):
    c, r = divmod(u, UNITS_PER_CHUNK)
    s, q = divmod(r, QUADS)
    return c, 32 * q + 2 * s


def field_row(f):
    s, q = divmod(f // 2, QUADS)
    return 32 * q + 2 * s + f % 2


DENSE_ROW = 2 * (COUPLES // QUADS)

EVACS = [("chunk", 0, 0), ("chunk", 1, 1), ("chunk", 2, 0), ("fields", CHUNKS, 0), ("chunk", 3, 1)]
N_EVACS = len(EVACS)
J1, J2 = N1 // P, N2 // P
MLP = J1 + J2 + 1


def tower_program(nc, dense_t, ids, tables, pair_k, w1, b1, w2, b2, w3, sums, out):
    f32, f32r, i32 = mybir.dt.float32, mybir.dt.float32r, mybir.dt.int32
    ACT = mybir.ActivationFunctionType
    ALU = mybir.AluOpType

    with ExitStack() as ctx:
        def sb(name, shape, dt):
            return ctx.enter_context(nc.sbuf_tensor(name, shape, dt))

        def sem(name):
            return ctx.enter_context(nc.semaphore(name))

        k_split = sb("k_split", [P, BLOCKS, DIM], f32r)
        x_hi = sb("x_hi", [P, 4, TILE], f32r)
        x_lo = sb("x_lo", [P, 4, TILE], f32r)
        xt = sb("xt", [P, COUPLES, TILE], f32)
        prod = sb("prod", [P, PROD_SLOTS, 2 * TILE], f32)
        rows = sb("rows", [P, GATHER_SLOTS, ROWSETS, 2, DIM], f32)
        twice = sb("twice", [P, 2, ROWSETS, 2, DIM], f32)
        sums_sb = sb("sums_sb", [P, TILE], f32)
        ids_now = sb("ids_now", [P, ROWSETS * FIELDS], i32)
        ones_strip = sb("ones_strip", [P, 62], f32)
        ident = sb("ident", [P, P], f32)
        b1_sb = sb("b1_sb", [P, J1], f32)
        b2_sb = sb("b2_sb", [P, J2], f32)
        w3_sb = sb("w3_sb", [P, J2], f32)

        xt_flat = xt[:, :, :].rearrange("p m b -> p (m b)")
        raw_cols = RAW_BLOCKS * DIM
        raw = [xt_flat[0:DIM, r * raw_cols:(r + 1) * raw_cols] for r in range(RAW_SLOTS)]
        h_in = xt[:, 0:5, :]
        w1_sb = xt[:, 5:10, :]
        h1 = xt[:, 10:14, :]
        h2 = xt[:, 14:16, :]
        w2_sb = prod[:, 0, :].rearrange("p (k n) -> p k n", k=J1)
        y_sb = prod[0:1, 1, 0:TILE]

        y_banks = [ctx.enter_context(nc.psum_tensor(f"y{i}", [P, 2, TILE], f32)) for i in range(Y_SLOTS)]
        acc = [ctx.enter_context(nc.psum_tensor(f"acc{i}", [P, TILE], f32)) for i in range(2)]
        mlp_bank = [y_banks[b // 2][:, b % 2, :] for b in range(6)] + [acc[0][0:1, :]]

        ids_loaded = sem("ids_loaded")
        ident_zeroed = sem("ident_zeroed")
        strip_zeroed = sem("strip_zeroed")
        consts_made = sem("consts_made")
        raw_loaded = [sem(f"raw_loaded{r}") for r in range(RAW_SLOTS)]
        k_high = sem("k_high")
        k_ready = sem("k_ready")
        doubled = sem("doubled")
        pool_passed = sem("pool_passed")
        gathered = [sem(f"gathered{s}") for s in range(GATHER_SLOTS)]
        y_full = sem("y_full")
        y_free = sem("y_free")
        x_copied = sem("x_copied")
        stack_ready = sem("stack_ready")
        summed = sem("summed")
        fields_summed = sem("fields_summed")
        acc_read = sem("acc_read")
        stored = sem("stored")
        weights_loaded = sem("weights_loaded")
        small_loaded = sem("small_loaded")
        h_loaded = sem("h_loaded")
        mlp_done = sem("mlp_done")
        mlp_read = sem("mlp_read")
        out_stored = sem("out_stored")

        block = ctx.enter_context(nc.Block())

        def before(t, n):
            return (t + 1) * n

        ROWS_IN = COUPLES // GATHER_SLOTS * ROWSETS * 2 * 16

        def double(act, t, k):
            s = k % GATHER_SLOTS
            act.wait_ge(gathered[s], ROWS_IN * t + (k // GATHER_SLOTS + 1) * (ROWSETS * 32))
            for h in (1, 0):
                nc.scalar.copy(twice[:, h, :, :, :],
                               rows[:, s, :, h:h + 1, :].to_broadcast([P, ROWSETS, 2, DIM])).then_inc(doubled, 1)

        def evac_after(e):
            kind, c, _ = EVACS[e]
            if kind == "fields":
                return FIELDS_AT + 3
            return (c + 1) * UNITS_PER_CHUNK // 2 + 2

        def drain(act, t, e):
            kind, c, bank = EVACS[e]
            if kind == "fields":
                act.wait_ge(fields_summed, t + 1)
            else:
                act.wait_ge(summed, before(t, N_GROUPS) + (c + 1) * GROUPS_PER_CHUNK)
            act.wait_ge(stored, 16 * (t * N_EVACS + e + 1))
            nc.scalar.copy(sums_sb[:], acc[bank][:]).then_inc(acc_read, 1)

        FIELDS_AT = next(j for j in range(N_PROD) if UNITS[2 * j][0] == 0 or UNITS[2 * j + 1][0] == 0)

        @block.gpsimd
        def _(pool):
            pool.memset(ident[:], 0.0).then_inc(ident_zeroed, 1)
            pool.wait_ge(ident_zeroed, 1)
            pool.affine_select(out=ident[:], in_=ident[:], compare_op=ALU.not_equal, fill=1.0, base=0,
                               pattern=[[-1, P]], channel_multiplier=1).then_inc(consts_made, 1)
            with pool.Fori(0, TILES) as t:
                pool.dma_start(ids_now[:], ids[:, bass.ds(t, 1), :].rearrange("p o n -> p (o n)")
                               ).then_inc(ids_loaded, 16)
                pool.wait_ge(ids_loaded, 16 * (t + 1))
                pool.sem_inc(pool_passed, 1)
                for k in range(COUPLES):
                    m = COUPLES - 1 - k
                    pool.wait_ge(doubled, before(t, FIELDS) + 2 * (k - GATHER_SLOTS) + 2)
                    pool.sem_inc(pool_passed, 1)
                    for h in (1, 0):
                        for c in range(ROWSETS):
                            f = 2 * m + h
                            pool.indirect_dma_start(
                                out=rows[:, k % GATHER_SLOTS, c, h, :], out_offset=None, in_=tables[f],
                                in_offset=bass.IndirectOffsetOnAxis(
                                    ap=ids_now[:, c * FIELDS + f:c * FIELDS + f + 1], axis=0)
                            ).then_inc(gathered[k % GATHER_SLOTS], 16)
                for s in range(GATHER_SLOTS):
                    pool.wait_ge(gathered[s], before(t, ROWS_IN))
                    pool.sem_inc(pool_passed, 1)

        @block.sync
        def _(sp):
            for r in range(RAW_CHUNKS):
                if r >= RAW_SLOTS:
                    sp.wait_ge(k_ready, r - RAW_SLOTS + 1)
                sp.dma_start(raw[r % RAW_SLOTS], pair_k[:, r * raw_cols:(r + 1) * raw_cols]
                             ).then_inc(raw_loaded[r % RAW_SLOTS], 16)
            sp.dma_start(b1_sb[:], b1).then_inc(small_loaded, 16)
            sp.dma_start(b2_sb[:], b2).then_inc(small_loaded, 16)
            sp.dma_start(w3_sb[:], w3).then_inc(small_loaded, 16)
            with sp.Fori(0, TILES) as t:
                for n, (_, c, _) in enumerate(EVACS):
                    sp.wait_ge(acc_read, before(t, N_EVACS) + n + 1)
                    sp.dma_start(sums[c, :, bass.ds(t * TILE, TILE)], sums_sb[:]
                                 ).then_inc(stored, 16)
            sp.wait_ge(y_free, (TILES + 1) * N_OPS)
            sp.wait_ge(summed, (TILES + 1) * N_GROUPS)
            sp.wait_ge(fields_summed, TILES)
            sp.dma_start(w1_sb, w1).then_inc(weights_loaded, 16)
            sp.dma_start(w2_sb, w2).then_inc(weights_loaded, 16)
            sp.wait_ge(stored, 16 * (TILES * N_EVACS + 1))
            with sp.Fori(0, TILES) as n:
                sp.wait_ge(mlp_done, n * MLP + J1)
                cols = bass.ds(n * TILE, TILE)
                lo, hi = DENSE_ROW, DENSE_ROW + DENSE
                sp.dma_start(h_in[:, 0:CHUNKS, :], sums[0:CHUNKS, :, cols].rearrange("c p b -> p c b")
                             ).then_inc(h_loaded, 16)
                sp.dma_start(h_in[0:lo, CHUNKS, :], sums[CHUNKS, 0:lo, cols]).then_inc(h_loaded, 16)
                sp.dma_start(h_in[lo:hi, CHUNKS, :], dense_t[:, cols]).then_inc(h_loaded, 16)
                sp.dma_start(h_in[hi:P, CHUNKS, :], sums[CHUNKS, hi:P, cols]).then_inc(h_loaded, 16)
                sp.wait_ge(mlp_read, before(n, MLP) + MLP)
                sp.dma_start(out[0:1, cols], y_sb).then_inc(out_stored, 16)
            sp.wait_ge(out_stored, 16 * (TILES + 1))

        @block.scalar
        def _(act):
            act.sem_inc(acc_read, N_EVACS)
            act.sem_inc(stored, 16)
            act.sem_inc(doubled, FIELDS)
            act.sem_inc(mlp_read, MLP)
            act.sem_inc(out_stored, 16)
            for r in range(RAW_CHUNKS):
                act.wait_ge(raw_loaded[r % RAW_SLOTS], 16 * (r // RAW_SLOTS + 1))
                nc.scalar.copy(k_split[0:DIM, r * RAW_BLOCKS:(r + 1) * RAW_BLOCKS, :],
                               raw[r % RAW_SLOTS].rearrange("p (k e) -> p k e", e=DIM)).then_inc(k_high, 1)
            act.wait_ge(k_ready, RAW_CHUNKS)
            with act.Fori(0, TILES) as t:
                evac = 0
                double(act, t, 0)
                for n, (kind, what) in enumerate(OPS):
                    if kind == "x":
                        m, k = what, COUPLES - 1 - what
                        if k == 0:
                            act.wait_ge(y_free, before(t, N_OPS))
                        act.wait_ge(y_full, before(t, N_OPS) + n + 1)
                        y = y_banks[n % Y_SLOTS]
                        for h in (1, 0):
                            part = slice(DIM * h, DIM * h + DIM)
                            nc.scalar.copy(x_hi[:, 2 * (m % 2) + h, :], y[:, h, :]).then_inc(x_copied, 1)
                            nc.scalar.copy(xt[part, m, :], y[part, h, :]).then_inc(x_copied, 1)
                        if k + 1 < COUPLES:
                            double(act, t, k + 1)
                    elif evac < N_EVACS and evac_after(evac) == what:
                        name, c, bank = EVACS[evac]
                        drain(act, t, evac)
                        evac += 1
                while evac < N_EVACS:
                    drain(act, t, evac)
                    evac += 1
            act.wait_ge(small_loaded, 48)
            with act.Fori(0, TILES) as n:
                for j in range(J1 + J2):
                    act.wait_ge(mlp_done, before(n, MLP) + j + 1)
                    dst, bias = (h1[:, j, :], b1_sb[:, j:j + 1]) if j < J1 else \
                        (h2[:, j - J1, :], b2_sb[:, j - J1:j - J1 + 1])
                    nc.scalar.activation(dst, mlp_bank[j], ACT.Relu, bias=bias).then_inc(mlp_read, 1)
                act.wait_ge(mlp_done, before(n, MLP) + MLP)
                act.wait_ge(out_stored, 16 * (n + 1))
                nc.scalar.copy(y_sb, mlp_bank[MLP - 1]).then_inc(mlp_read, 1)

        @block.vector
        def _(dve):
            dve.memset(ones_strip[:], 0.0).then_inc(strip_zeroed, 1)
            dve.wait_ge(strip_zeroed, 1)
            dve.memset(ones_strip[0:DIM, 30:31], 1.0).then_inc(consts_made, 1)
            dve.memset(ones_strip[DIM:P, 31:32], 1.0).then_inc(consts_made, 1)
            dve.sem_inc(y_free, N_OPS)
            for r in range(RAW_CHUNKS):
                cols = slice(r * RAW_BLOCKS, (r + 1) * RAW_BLOCKS)
                dve.wait_ge(k_high, r + 1)
                nc.vector.tensor_tensor(k_split[DIM:P, cols, :],
                                        raw[r % RAW_SLOTS].rearrange("p (k e) -> p k e", e=DIM),
                                        k_split[0:DIM, cols, :], ALU.subtract).then_inc(k_ready, 1)
            with dve.Fori(0, TILES) as t:
                for n, (kind, what) in enumerate(OPS):
                    y = y_banks[n % Y_SLOTS]
                    if kind == "x":
                        m, k = what, COUPLES - 1 - what
                        for a, h in enumerate((1, 0)):
                            dve.wait_ge(x_copied, 4 * (COUPLES * t + k) + 2 * a + 2)
                            slot = 2 * (m % 2) + h
                            ins = nc.vector.tensor_tensor(x_lo[:, slot, :], y[:, h, :],
                                                          x_hi[:, slot, :], ALU.subtract)
                            ins.then_inc(stack_ready, 1)
                        dve.wait_ge(stack_ready, 2 * (COUPLES * t + k) + 2)
                        dve.sem_inc(y_free, 1)
                    else:
                        j = what
                        dve.wait_ge(y_full, before(t, N_OPS) + n + 1)
                        dve.wait_ge(summed, before(t, N_GROUPS) + (j - PROD_SLOTS) // 2 + 1)
                        m0, m1 = UNITS[2 * j][1], UNITS[2 * j + 1][1]
                        x = xt[:, m0:m0 + 2, :] if m1 > m0 else \
                            xt[:, m0:m0 + 1, :].to_broadcast([P, 2, TILE])
                        nc.vector.tensor_tensor(prod[:, j % PROD_SLOTS, :].rearrange("p (a b) -> p a b", a=2),
                                                y[:, :, :], x, ALU.mult).then_inc(y_free, 1)

        @block.tensor
        def _(pe):
            pe.sem_inc(y_full, N_OPS)
            pe.sem_inc(summed, N_GROUPS)
            pe.sem_inc(mlp_done, MLP)
            pe.wait_ge(consts_made, 3)

            def sum_group(t, g):
                c, s = divmod(g, GROUPS_PER_CHUNK)
                bank = acc[c % 2]
                if s == 0:
                    e = next(e for e, x in enumerate(EVACS) if x[:2] == ("chunk", c))
                    same = [a for a in range(e) if EVACS[a][2] == EVACS[e][2]]
                    prev = same[-1] if same else \
                        max(a for a in range(N_EVACS) if EVACS[a][2] == EVACS[e][2]) - N_EVACS
                    pe.wait_ge(acc_read, before(t, N_EVACS) + prev + 1)
                pe.wait_ge(y_free, before(t, N_OPS) + op_at("u", 2 * g + 1) + 1)
                for q in range(QUADS):
                    last = nc.tensor.matmul(
                        bank[32 * q:32 * q + 32, :], ones_strip[:, 30 - 2 * s:62 - 2 * s],
                        prod[:, (2 * g + q // 2) % PROD_SLOTS, (q % 2) * TILE:(q % 2 + 1) * TILE],
                        start=s == 0, stop=s == GROUPS_PER_CHUNK - 1)
                last.then_inc(summed, 1)

            def sum_fields(t):
                pe.wait_ge(stack_ready, 2 * COUPLES * (t + 1))
                pe.wait_ge(acc_read, before(t, N_EVACS) + 3)
                for s in range(COUPLES // QUADS):
                    for q in range(QUADS):
                        last = nc.tensor.matmul(acc[0][32 * q:32 * q + 32, :],
                                                ones_strip[:, 30 - 2 * s:62 - 2 * s],
                                                xt[:, QUADS * s + q, :],
                                                start=s == 0, stop=s == COUPLES // QUADS - 1)
                last.then_inc(fields_summed, 1)

            with pe.Fori(0, TILES) as t:
                seen = set()
                next_group = 0
                for n, (kind, what) in enumerate(OPS):
                    y = y_banks[n % Y_SLOTS]
                    if kind == "u" and what == FIELDS_AT:
                        sum_fields(t)
                    slot_free = before(t, N_OPS) + n - Y_SLOTS + 1
                    if kind == "x":
                        m, k = what, COUPLES - 1 - what
                        pe.wait_ge(y_free, slot_free)
                        for h in (1, 0):
                            pe.wait_ge(doubled, before(t, FIELDS) + 2 * k + 2 - h)
                            for c in range(ROWSETS):
                                last = nc.tensor.transpose(
                                    y[:, h, P * c:P * c + P],
                                    twice[:, h, c, :, :].rearrange("p a d -> p (a d)"), ident[:])
                        last.then_inc(y_full, 1)
                        continue
                    j = what
                    pe.wait_ge(y_free, slot_free)
                    for a in range(2):
                        u = 2 * j + a
                        i, m = UNITS[u]
                        if i not in seen:
                            seen.add(i)
                            k = COUPLES - 1 - i // 2
                            pe.wait_ge(stack_ready, 2 * (COUPLES * t + k) + (1 if i % 2 else 2))
                        pe.wait_ge(k_ready, 2 * u // RAW_BLOCKS + 1)
                        k_unit = k_split[:, 2 * u:2 * u + 2, :].rearrange("p a e -> p (a e)")
                        slot = 2 * (i // 2 % 2) + i % 2
                        nc.tensor.matmul(y[:, a, :], k_unit, x_hi[:, slot, :], start=True, stop=False)
                        last = nc.tensor.matmul(y[:, a, :], k_unit, x_lo[:, slot, :], start=False, stop=True)
                    last.then_inc(y_full, 1)
                    if j % 2 == 1 and j >= 3:
                        sum_group(t, next_group)
                        next_group += 1
                while next_group < N_GROUPS:
                    sum_group(t, next_group)
                    next_group += 1

            pe.wait_ge(y_free, (TILES + 1) * N_OPS)
            pe.wait_ge(acc_read, (TILES + 1) * N_EVACS)
            pe.wait_ge(weights_loaded, 32)
            pe.wait_ge(small_loaded, 48)
            with pe.Fori(0, TILES) as n:
                pe.wait_ge(h_loaded, 64 * (n + 1))
                for j in range(J1):
                    pe.wait_ge(mlp_read, n * MLP + j + 1)
                    for c in range(CHUNKS + 1):
                        last = nc.tensor.matmul(mlp_bank[j], w1_sb[:, c, j * P:(j + 1) * P], h_in[:, c, :],
                                                start=c == 0, stop=c == CHUNKS)
                    last.then_inc(mlp_done, 1)
                pe.wait_ge(mlp_read, before(n, MLP) + J1)
                for j in range(J2):
                    for c in range(J1):
                        last = nc.tensor.matmul(mlp_bank[J1 + j], w2_sb[:, c, j * P:(j + 1) * P], h1[:, c, :],
                                                start=c == 0, stop=c == J1 - 1)
                    last.then_inc(mlp_done, 1)
                pe.wait_ge(mlp_read, before(n, MLP) + J1 + J2)
                for c in range(J2):
                    last = nc.tensor.matmul(mlp_bank[MLP - 1], w3_sb[:, c:c + 1], h2[:, c, :],
                                            start=c == 0, stop=c == J2 - 1)
                last.then_inc(mlp_done, 1)


def kernel(**inputs):
    import numpy as np
    import concourse.bacc as bacc
    from concourse.bass_utils import run_bass_kernel_spmd

    f32 = mybir.dt.float32
    nc = bacc.Bacc("TRN2", target_bir_lowering=False, num_devices=1)
    arrays = {}

    def dram_in(name, a):
        a = np.ascontiguousarray(a)
        arrays[name] = a
        return nc.dram_tensor(name, a.shape, mybir.dt.from_np(a.dtype), kind="ExternalInput").ap()

    ids = np.asarray(inputs["ids"]).reshape(TILES, ROWSETS, P, FIELDS).transpose(2, 0, 1, 3)
    ids = ids.reshape(P, TILES, ROWSETS * FIELDS)
    index = {}
    for i in range(FIELDS):
        for j in range(i + 1, FIELDS):
            index[(i, j)] = len(index)
    pair_k = np.asarray(inputs["L0_rec_kernels"])
    k = np.zeros((DIM, BLOCKS, DIM), pair_k.dtype)
    w_top1 = np.asarray(inputs["W_top1"])
    w1 = np.zeros((CHUNKS + 1, P, N1), w_top1.dtype)
    for u, (i, m) in enumerate(UNITS):
        c, row = z_row(u)
        for h in ((1,) if single((i, m)) else (0, 1)):
            k[:, 2 * u + h] = pair_k[index[(i, 2 * m + h)]]
            w1[c, row + h] = w_top1[FIELDS + index[(i, 2 * m + h)]]
    for f in range(FIELDS):
        w1[CHUNKS, field_row(f)] = w_top1[f]
    w1[CHUNKS, DENSE_ROW:DENSE_ROW + DENSE] = w_top1[FIELDS + PAIRS:]

    args = [
        dram_in("dense_t", np.asarray(inputs["dense_ctx"]).T),
        dram_in("ids", ids),
        [dram_in(f"tbl_{f}", np.asarray(inputs[f"tbl_{f}"])) for f in range(FIELDS)],
        dram_in("pair_k", k.reshape(DIM, BLOCKS * DIM)),
        dram_in("w1", w1.transpose(1, 0, 2)),
        dram_in("b1", np.asarray(inputs["b_top1"]).reshape(J1, P).T),
        dram_in("w2", np.asarray(inputs["W_top2"]).reshape(J1, P, N2).transpose(1, 0, 2)),
        dram_in("b2", np.asarray(inputs["b_top2"]).reshape(J2, P).T),
        dram_in("w3", np.asarray(inputs["W_top3"]).reshape(J2, P).T),
        nc.dram_tensor("sums", (CHUNKS + 1, P, BATCH), f32).ap(),
        nc.dram_tensor("out", (1, BATCH), f32, kind="ExternalOutput").ap(),
    ]
    tower_program(nc, *args)
    r = run_bass_kernel_spmd(nc, [arrays], core_ids=[0])
    return r.results[0]["out"].reshape(BATCH, 1)
```

```python
import concourse.bass as bass
from concourse import mybir
from contextlib import ExitStack, nullcontext

P = 128
BATCH, FIELDS, DIM = 2048, 32, 64
DENSE = 16
N1, N2 = 512, 256
COUPLES = FIELDS // 2
FIELD_QUADS = FIELDS // 4
TILE = 512
TILES = BATCH // TILE
ROWSETS = TILE // P
GATHER_SLOTS = 4
Y_SLOTS = 2
X_BANKS = 3
PROD_SLOTS = 4
QUADS = 4
STACK_SLOTS = 4
UNITS_PER_CHUNK = 64
RAW_CHUNKS = 16
RAW_SLOTS = 4
RAW_EARLY = 8
RAW_LATE_SLOTS = 2


def interaction_units():
    units = []
    for quad in range(FIELD_QUADS - 1, -1, -1):
        a, b, c, d = range(4 * quad, 4 * quad + 4)
        above = range(COUPLES - 1, 2 * quad + 1, -1)
        units += [(i, m) for i in (d, c, b) for m in above]
        units += [(b, COUPLES), (c, COUPLES + 1)]
        units += [(a, m) for m in (*above, 2 * quad + 1)]
    for j in range(0, len(units), 2):
        if units[j][1] > units[j + 1][1]:
            units[j], units[j + 1] = units[j + 1], units[j]
    return units


def couple_fields(i, m):
    first = 4 * (i // 4)
    if m == COUPLES:
        return first, first + 3
    if m == COUPLES + 1:
        return first + 1, first + 3
    return 2 * m, 2 * m + 1


UNITS = interaction_units()
PAIRS = FIELDS * (FIELDS - 1) // 2
BLOCKS = 2 * len(UNITS)
CHUNKS = -(-len(UNITS) // UNITS_PER_CHUNK)
RAW_BLOCKS = BLOCKS // RAW_CHUNKS


def last_product(wanted):
    return max(u // 2 for u, unit in enumerate(UNITS) if wanted(*unit))


def last_of_step(i):
    return last_product(lambda a, _: a == i)


def last_of_couple(m):
    return last_product(lambda a, b: b == m or b >= COUPLES and a // 4 == m // 2)


def last_of_quad(quad):
    return last_product(lambda a, b: a // 4 == quad and b >= COUPLES)


def first_of_step(i):
    return min(u for u, unit in enumerate(UNITS) if unit[0] == i) // 2


def stack_slot(f):
    return STACK_SLOTS - 1 if f == 0 else (FIELDS - 2 - f) % STACK_SLOTS


def slot_before(f):
    g = f + 1
    while g % FIELDS == FIELDS - 1 or stack_slot(g % FIELDS) != stack_slot(f):
        g += 1
    return g if g < FIELDS else g - 2 * FIELDS


N_PROD = len(UNITS) // 2
N_GROUPS = N_PROD // 2
GROUPS_PER_CHUNK = UNITS_PER_CHUNK // QUADS
FIELDS_AT = first_of_step(0)
AHEAD = 6
RAW_STARTED = RAW_EARLY + AHEAD
SHORT_STEPS = 16
assert N_PROD % Y_SLOTS == 0 and N_PROD % PROD_SLOTS == 0 and (FIELDS + 1) % X_BANKS == 0


def plan():
    first = FIELDS - 1 - STACK_SLOTS
    lows, extras = {}, []

    def low_after(j, latest):
        if j < SHORT_STEPS:
            return j
        after = j + 1 + j % 2
        while lows.get(after):
            after += 2
        return max(j, min(after, latest))

    order = [("high", first), ("low", first)]
    group = 0
    for j in range(N_PROD):
        if j == FIELDS_AT:
            order.append(("fields",))
        order.append(("product", j))
        if j % 2 == 0 and j // 2 < RAW_CHUNKS - RAW_STARTED:
            order.append(("split k", RAW_STARTED + j // 2))
        if j == FIELDS_AT + 1:
            order.append(("read fields",))
        for i in range(FIELDS - 2, 0, -1):
            if max(map(last_of_step, range(i, FIELDS - 1))) == j:
                for f in range(first - 1, -1, -1):
                    if slot_before(f) == i:
                        order.append(("high", f))
                        lows.setdefault(low_after(j, first_of_step(f) - 1), []).append(f)
                if i - 5 >= 0:
                    for pending in lows.values():
                        if i - 5 + X_BANKS in pending:
                            pending.remove(i - 5 + X_BANKS)
                            order.append(("low", i - 5 + X_BANKS))
                    order.append(("transpose", i - 5))
                if i == FIELDS - 3:
                    order.append(("extra", FIELD_QUADS - 2))
                elif i % 4 == 3 and i // 4 < FIELD_QUADS - 2:
                    extras.append(("extra", i // 4))
        order += [("low", f) for f in lows.pop(j, ())]
        if j % 2 == 1 and j >= 3:
            order.append(("sum", group))
            group += 1
            order += extras
            extras = []
        for n, step in enumerate((1, 2, 3, 4, 6)):
            if j == FIELDS_AT + step:
                f = 2 * FIELDS - 1 - n
                order.append(("transpose", f))
                if 1 <= n < STACK_SLOTS:
                    order.append(("high", f))
                    lows.setdefault(low_after(j, N_PROD - 1), []).append(f)
                if n == 3:
                    order.append(("extra", 2 * FIELD_QUADS - 1))
    order.append(("transpose", 2 * FIELDS - AHEAD))
    order.append(("sum", group))
    assert not lows
    return order


ORDER = plan()


def z_row(u):
    c, r = divmod(u, UNITS_PER_CHUNK)
    s, q = divmod(r, QUADS)
    return c, 32 * q + 2 * s


def field_row(f):
    s, q = divmod(f // 2, QUADS)
    return 32 * q + 2 * s + f % 2


def ends_chunk(g):
    return g % GROUPS_PER_CHUNK == GROUPS_PER_CHUNK - 1 or g == N_GROUPS - 1


DENSE_ROW = 2 * (COUPLES // QUADS)

EVACS = [*range(CHUNKS - 1), CHUNKS, CHUNKS - 1]
N_EVACS = len(EVACS)
J1, J2 = N1 // P, N2 // P
MLP_STEPS = [(layer, b, j) for layer, n in ((1, J1), (2, J2), (3, 1)) for b in range(2) for j in range(n)]
MLP = len(MLP_STEPS)
MLP_PASSES = TILES // 2


def mlp_at(layer, b, j):
    return MLP_STEPS.index((layer, b, j))


def tower_program(nc, dense_t, ids, tables, pair_k, w1, b1, w2, b2, w3, sums, out):
    f32, f32r, i32 = mybir.dt.float32, mybir.dt.float32r, mybir.dt.int32
    ACT = mybir.ActivationFunctionType
    ALU = mybir.AluOpType

    with ExitStack() as ctx:
        def sb(name, shape, dt):
            return ctx.enter_context(nc.sbuf_tensor(name, shape, dt))

        def bank(name, shape):
            return ctx.enter_context(nc.psum_tensor(name, shape, f32))

        def sem(name):
            return ctx.enter_context(nc.semaphore(name))

        k_split = sb("k_split", [P, BLOCKS, DIM], f32r)
        x_hi = sb("x_hi", [P, STACK_SLOTS, TILE], f32r)
        x_lo = sb("x_lo", [P, STACK_SLOTS, TILE], f32r)
        xt = sb("xt", [P, COUPLES + 2, TILE], f32)
        prod = sb("prod", [P, PROD_SLOTS, 2 * TILE], f32)
        rows = sb("rows", [P, GATHER_SLOTS, ROWSETS, 2, DIM], f32)
        twice = sb("twice", [P, 2, ROWSETS, 2, DIM], f32)
        sums_sb = sb("sums_sb", [P, TILE], f32)
        ids_now = sb("ids_now", [P, ROWSETS * FIELDS], i32)
        ones_strip = sb("ones_strip", [P, 62], f32)
        ident = sb("ident", [P, P], f32)
        b1_sb = sb("b1_sb", [P, J1], f32)
        b2_sb = sb("b2_sb", [P, J2], f32)
        w3_sb = sb("w3_sb", [P, J2], f32)

        xt_flat = xt[:, :, :].rearrange("p m b -> p (m b)")
        raw_cols = RAW_BLOCKS * DIM
        raw = [xt_flat[0:DIM, r * raw_cols:(r + 1) * raw_cols].rearrange("p (k e) -> p k e", e=DIM)
               for r in range(RAW_SLOTS)]
        prod_flat = prod[:, :, :].rearrange("p s b -> p (s b)").rearrange("p (s b) -> p s b", b=TILE)
        rows_flat = rows[:, :, :, :, :].rearrange("p s c h d -> p (s c h d)").rearrange(
            "p (s b) -> p s b", b=TILE)
        w1_sb = xt[:, COUPLES - CHUNKS - 1:COUPLES, :]
        w2_sb = twice[:, :, :, :, :].rearrange("p h c a d -> p (h c a d)").rearrange("p (k n) -> p k n", k=J1)
        h_in_first = COUPLES - 2 * (CHUNKS + 1)
        h_in = [xt[:, h_in_first:h_in_first + CHUNKS + 1, :], prod_flat[:, 0:CHUNKS + 1, :]]
        h1 = [xt[:, J2:J2 + J1, :], rows_flat]
        h2 = [xt[:, 0:J2, :], prod_flat[:, CHUNKS + 1:CHUNKS + 1 + J2, :]]
        y_sb = [prod_flat[0:1, CHUNKS + 1 + J2, :], sums_sb[0:1, :]]

        y_banks = [bank(f"y{i}", [P, 2, TILE]) for i in range(Y_SLOTS)]
        acc = bank("acc", [P, TILE])
        x_banks = [bank(f"x{i}", [P, TILE]) for i in range(X_BANKS)]
        mlp_bank = [y_banks[b // 2][:, b % 2, :] for b in range(2 * Y_SLOTS)] + \
            [x[:] for x in x_banks] + [acc[:]]

        ids_loaded = sem("ids_loaded")
        ident_zeroed = sem("ident_zeroed")
        strip_zeroed = sem("strip_zeroed")
        consts_made = sem("consts_made")
        raw_loaded = [sem(f"raw_loaded{r}") for r in range(RAW_SLOTS)]
        k_high = sem("k_high")
        k_ready = sem("k_ready")
        pool_passed = sem("pool_passed")
        act_passed = sem("act_passed")
        gathered = [sem(f"gathered{s}") for s in range(GATHER_SLOTS)]
        doubled = sem("doubled")
        transposed = sem("transposed")
        xt_copied = sem("xt_copied")
        high_made = sem("high_made")
        extra_made = sem("extra_made")
        x_free = sem("x_free")
        y_full = sem("y_full")
        y_free = sem("y_free")
        summed = sem("summed")
        fields_summed = sem("fields_summed")
        acc_read = sem("acc_read")
        stored = sem("stored")
        small_loaded = sem("small_loaded")
        weights_loaded = sem("weights_loaded")
        h_loaded = [sem(f"h_loaded{b}") for b in range(2)]
        mlp_done = sem("mlp_done")
        mlp_read = sem("mlp_read")
        out_stored = [sem(f"out_stored{b}") for b in range(2)]

        block = ctx.enter_context(nc.Block())

        def before(t, n):
            return (t + 1) * n

        ROWS_IN = COUPLES // GATHER_SLOTS * ROWSETS * 2 * 16

        def raw_slot(r):
            if r < RAW_EARLY:
                return r % RAW_SLOTS, r // RAW_SLOTS
            s = (r - RAW_EARLY) % RAW_LATE_SLOTS
            return s, RAW_EARLY // RAW_SLOTS + (r - RAW_EARLY) // RAW_LATE_SLOTS

        def nth(f):
            return FIELDS - 1 - f

        X_USES = FIELDS

        def freed(t, f):
            return X_USES * t + nth(f)

        def in_tile(t, f):
            return (t, f) if f < FIELDS else (t + 1, f - FIELDS)

        def guard(engine, t, f):
            return engine.If(t < TILES - 1) if f >= FIELDS else nullcontext()

        @block.gpsimd
        def _(pool):
            pool.memset(ident[:], 0.0).then_inc(ident_zeroed, 1)
            pool.wait_ge(ident_zeroed, 1)
            pool.affine_select(out=ident[:], in_=ident[:], compare_op=ALU.not_equal, fill=1.0, base=0,
                               pattern=[[-1, P]], channel_multiplier=1).then_inc(consts_made, 1)
            with pool.Fori(0, TILES) as t:
                pool.dma_start(ids_now[:], ids[:, bass.ds(t, 1), :].rearrange("p o n -> p (o n)")
                               ).then_inc(ids_loaded, 16)
                pool.wait_ge(ids_loaded, 16 * (t + 1))
                pool.sem_inc(pool_passed, 1)
                for k in range(COUPLES):
                    m, s = COUPLES - 1 - k, k % GATHER_SLOTS
                    pool.wait_ge(doubled, before(t, FIELDS) + 2 * (k - GATHER_SLOTS) + 2)
                    pool.sem_inc(pool_passed, 1)
                    for h in (1, 0):
                        for c in range(ROWSETS):
                            f = 2 * m + h
                            pool.indirect_dma_start(
                                out=rows[:, s, c, h, :], out_offset=None, in_=tables[f],
                                in_offset=bass.IndirectOffsetOnAxis(
                                    ap=ids_now[:, c * FIELDS + f:c * FIELDS + f + 1], axis=0)
                            ).then_inc(gathered[s], 16)
                for s in range(GATHER_SLOTS):
                    pool.wait_ge(gathered[s], before(t, ROWS_IN))
                    pool.sem_inc(pool_passed, 1)

        @block.sync
        def _(sp):
            for r in range(RAW_CHUNKS):
                s, used = raw_slot(r)
                if used:
                    sp.wait_ge(k_ready, max(q for q in range(r) if raw_slot(q)[0] == s) + 1)
                sp.dma_start(raw[s],
                             pair_k[:, r * raw_cols:(r + 1) * raw_cols].rearrange("p (k e) -> p k e", e=DIM)
                             ).then_inc(raw_loaded[s], 16)
            sp.dma_start(b1_sb[:], b1).then_inc(small_loaded, 16)
            sp.dma_start(b2_sb[:], b2).then_inc(small_loaded, 16)
            sp.dma_start(w3_sb[:], w3).then_inc(small_loaded, 16)

            def store_sums(t, n):
                if EVACS[n] == CHUNKS:
                    sp.wait_ge(x_free, X_USES * (t + 1))
                else:
                    sp.wait_ge(acc_read, before(t, CHUNKS) + EVACS[n] + 1)
                sp.dma_start(sums[EVACS[n], :, bass.ds(t * TILE, TILE)], sums_sb[:]).then_inc(stored, 16)

            with sp.Fori(0, TILES - 1) as t:
                for n in range(N_EVACS):
                    store_sums(t, n)
            t = TILES - 1
            for n in range(N_EVACS - 1):
                store_sums(t, n)
            sp.wait_ge(transposed, TILES * FIELDS)
            sp.dma_start(w2_sb, w2).then_inc(weights_loaded, 16)
            sp.wait_ge(y_free, before(t, N_PROD) + last_of_couple(COUPLES - CHUNKS - 1) + 1)
            sp.dma_start(w1_sb, w1).then_inc(weights_loaded, 16)

            def load_h(n, b):
                cols = bass.ds(n * TILE, TILE)
                lo, hi = DENSE_ROW, DENSE_ROW + DENSE
                sp.dma_start(h_in[b][:, 0:CHUNKS, :], sums[0:CHUNKS, :, cols].rearrange("c p b -> p c b")
                             ).then_inc(h_loaded[b], 16)
                sp.dma_start(h_in[b][0:lo, CHUNKS, :], sums[CHUNKS, 0:lo, cols]).then_inc(h_loaded[b], 16)
                sp.dma_start(h_in[b][lo:hi, CHUNKS, :], dense_t[:, cols]).then_inc(h_loaded[b], 16)
                sp.dma_start(h_in[b][hi:P, CHUNKS, :], sums[CHUNKS, hi:P, cols]).then_inc(h_loaded[b], 16)

            sp.wait_ge(y_free, before(t, N_PROD) + last_of_couple(h_in_first) + 1)
            sp.wait_ge(stored, 16 * (N_EVACS + 1))
            load_h(0, 0)
            store_sums(t, N_EVACS - 1)
            sp.wait_ge(summed, before(t, N_GROUPS) + N_GROUPS)
            sp.wait_ge(stored, 16 * (TILES * N_EVACS + 1))
            load_h(1, 1)
            with sp.Fori(1, MLP_PASSES) as i:
                for b in range(2):
                    sp.wait_ge(mlp_done, i * MLP + mlp_at(1, b, J1 - 1) + 1)
                    load_h(2 * i + b, b)

        @block.scalar
        def _(act):
            act.sem_inc(acc_read, CHUNKS)
            act.sem_inc(stored, 16)
            act.sem_inc(doubled, FIELDS)
            act.sem_inc(mlp_read, MLP)
            for b in range(2):
                act.sem_inc(out_stored[b], 16)

            def double(t, f):
                k, s = nth(f) // 2, nth(f) // 2 % GATHER_SLOTS
                act.wait_ge(gathered[s], ROWS_IN * t + (k // GATHER_SLOTS + 1) * (ROWSETS * 32))
                nc.scalar.copy(twice[:, f % 2, :, :, :],
                               rows[:, s, :, f % 2:f % 2 + 1, :].to_broadcast([P, ROWSETS, 2, DIM])
                               ).then_inc(doubled, 1)

            def copy_field(t, f):
                act.wait_ge(transposed, FIELDS * t + nth(f) + 1)
                act.wait_ge(y_free, before(t, N_PROD) - N_PROD + last_of_couple(f // 2) + 1)
                part = slice(DIM * (f % 2), DIM * (f % 2) + DIM)
                nc.scalar.copy(xt[part, f // 2, :], x_banks[nth(f) % X_BANKS][part, :]).then_inc(xt_copied, 1)

            def make_high(t, f):
                g = slot_before(f)
                act.wait_ge(y_full, before(t, N_PROD) + (last_of_step(g) if g >= 0 else
                                                         last_of_step(g + FIELDS) - N_PROD) + 1)
                nc.scalar.copy(x_hi[:, stack_slot(f), :], x_banks[nth(f) % X_BANKS][:]
                               ).then_inc(high_made, 1)

            def make_extra(t, quad):
                last = last_of_quad(quad + 1) if quad < FIELD_QUADS - 1 else last_of_quad(0) - N_PROD
                act.wait_ge(y_free, before(t, N_PROD) + last + 1)
                act.wait_ge(xt_copied, FIELDS * t + nth(4 * quad) + 1)
                nc.scalar.copy(xt[0:DIM, COUPLES, :], xt[0:DIM, 2 * quad, :]).then_inc(extra_made, 1)
                nc.scalar.copy(xt[0:DIM, COUPLES + 1, :], xt[DIM:P, 2 * quad, :]).then_inc(extra_made, 1)
                nc.scalar.copy(xt[DIM:P, COUPLES:COUPLES + 2, :],
                               xt[DIM:P, 2 * quad + 1:2 * quad + 2, :].to_broadcast([DIM, 2, TILE])
                               ).then_inc(extra_made, 1)

            def k_high_part(r):
                s, used = raw_slot(r)
                act.wait_ge(raw_loaded[s], 16 * (used + 1))
                nc.scalar.copy(k_split[0:DIM, r * RAW_BLOCKS:(r + 1) * RAW_BLOCKS, :], raw[s]
                               ).then_inc(k_high, 1)

            for r in range(RAW_EARLY):
                k_high_part(r)
            double(0, FIELDS - 1)
            double(0, FIELDS - 2)
            act.wait_ge(k_ready, RAW_EARLY)
            for f in range(FIELDS - 1, FIELDS - 1 - AHEAD, -1):
                copy_field(0, f)
                double(0, f - 2)
                if FIELDS - 1 > f >= FIELDS - STACK_SLOTS:
                    make_high(0, f)
                if f == FIELDS - STACK_SLOTS:
                    make_extra(0, FIELD_QUADS - 1)
                k_high_part(RAW_EARLY + nth(f))
            with act.Fori(0, TILES) as t:
                for what in ORDER:
                    if what[0] == "transpose":
                        f = what[1]
                        with guard(act, t, f):
                            copy_field(*in_tile(t, f))
                        with guard(act, t, f if f >= 2 else FIELDS):
                            double(*in_tile(t, f - 2 if f >= 2 else f - 2 + 2 * FIELDS))
                    elif what[0] == "split k":
                        with act.If(t < 1):
                            k_high_part(what[1])
                            if what[1] == RAW_CHUNKS - 1:
                                act.wait_ge(k_ready, RAW_CHUNKS)
                                act.sem_inc(act_passed, 1)
                    elif what[0] == "extra":
                        with guard(act, t, 4 * what[1]):
                            make_extra(*((t, what[1]) if what[1] < FIELD_QUADS else
                                         (t + 1, what[1] - FIELD_QUADS)))
                    elif what[0] == "high":
                        with guard(act, t, what[1]):
                            make_high(*in_tile(t, what[1]))
                    elif what[0] == "sum" and ends_chunk(what[1]):
                        act.wait_ge(summed, before(t, N_GROUPS) + what[1] + 1)
                        n = EVACS.index(what[1] // GROUPS_PER_CHUNK)
                        act.wait_ge(stored, 16 * (t * N_EVACS + n + 1))
                        nc.scalar.copy(sums_sb[:], acc[:]).then_inc(acc_read, 1)
            act.wait_ge(y_free, before(TILES - 1, N_PROD) + N_PROD)
            act.wait_ge(summed, before(TILES - 1, N_GROUPS) + N_GROUPS)
            act.wait_ge(stored, 16 * (TILES * N_EVACS + 1))
            act.wait_ge(small_loaded, 48)
            with act.Fori(0, MLP_PASSES) as i:
                for n, (layer, b, j) in enumerate(MLP_STEPS):
                    act.wait_ge(mlp_done, before(i, MLP) + n + 1)
                    src = mlp_bank[n % 8]
                    if layer == 1:
                        nc.scalar.activation(h1[b][:, j, :], src, ACT.Relu, bias=b1_sb[:, j:j + 1]
                                             ).then_inc(mlp_read, 1)
                    elif layer == 2:
                        nc.scalar.activation(h2[b][:, j, :], src, ACT.Relu, bias=b2_sb[:, j:j + 1]
                                             ).then_inc(mlp_read, 1)
                    else:
                        act.wait_ge(out_stored[b], 16 * (i + 1))
                        nc.scalar.copy(y_sb[b], src[0:1, :]).then_inc(mlp_read, 1)
                        act.wait_ge(mlp_read, before(i, MLP) + n + 1)
                        act.dma_start(out[0:1, bass.ds((2 * i + b) * TILE, TILE)], y_sb[b]
                                      ).then_inc(out_stored[b], 16)
            for b in range(2):
                act.wait_ge(out_stored[b], 16 * (MLP_PASSES + 1))

        @block.vector
        def _(dve):
            dve.memset(ones_strip[:], 0.0).then_inc(strip_zeroed, 1)
            dve.wait_ge(strip_zeroed, 1)
            dve.memset(ones_strip[0:DIM, 30:31], 1.0).then_inc(consts_made, 1)
            dve.memset(ones_strip[DIM:P, 31:32], 1.0).then_inc(consts_made, 1)
            dve.sem_inc(y_free, N_PROD)

            def k_low_part(r):
                blocks = slice(r * RAW_BLOCKS, (r + 1) * RAW_BLOCKS)
                dve.wait_ge(k_high, r + 1)
                nc.vector.tensor_tensor(k_split[DIM:P, blocks, :], raw[raw_slot(r)[0]],
                                        k_split[0:DIM, blocks, :], ALU.subtract).then_inc(k_ready, 1)

            for r in range(RAW_EARLY):
                k_low_part(r)

            def make_low(t, f):
                x = x_banks[nth(f) % X_BANKS]
                dve.wait_ge(xt_copied, FIELDS * t + nth(f) + 1)
                dve.wait_ge(high_made, (FIELDS - 1) * t + nth(f))
                nc.vector.tensor_tensor(x_lo[:, stack_slot(f), :], x[:], x_hi[:, stack_slot(f), :],
                                        ALU.subtract).then_inc(x_free, 1)

            def multiply(t, j):
                dve.wait_ge(y_full, before(t, N_PROD) + j + 1)
                dve.wait_ge(summed, before(t, N_GROUPS) + (j - PROD_SLOTS) // 2 + 1)
                for a, m in UNITS[2 * j:2 * j + 2]:
                    if m >= COUPLES:
                        dve.wait_ge(extra_made, 3 * (FIELD_QUADS * t + FIELD_QUADS - a // 4))
                m0, m1 = UNITS[2 * j][1], UNITS[2 * j + 1][1]
                x = xt[:, m0:m1 + 1:m1 - m0, :] if m1 > m0 else xt[:, m0:m0 + 1, :].to_broadcast([P, 2, TILE])
                nc.vector.tensor_tensor(prod[:, j % PROD_SLOTS, :].rearrange("p (a b) -> p a b", a=2),
                                        y_banks[j % Y_SLOTS][:, :, :], x, ALU.mult).then_inc(y_free, 1)

            def read_fields(t):
                dve.wait_ge(fields_summed, t + 1)
                dve.wait_ge(stored, 16 * (t * N_EVACS + CHUNKS))
                nc.vector.tensor_copy(sums_sb[:], x_banks[FIELDS % X_BANKS][:]).then_inc(x_free, 1)

            for f in range(FIELDS - 1, FIELDS - 1 - AHEAD, -1):
                if FIELDS - 1 > f >= FIELDS - STACK_SLOTS:
                    make_low(0, f)
                k_low_part(RAW_EARLY + nth(f))
            with dve.Fori(0, TILES) as t:
                for what in ORDER:
                    if what[0] == "product":
                        multiply(t, what[1])
                    elif what[0] == "read fields":
                        read_fields(t)
                    elif what[0] == "split k":
                        with dve.If(t < 1):
                            k_low_part(what[1])
                    elif what[0] == "low":
                        with guard(dve, t, what[1]):
                            make_low(*in_tile(t, what[1]))

        @block.tensor
        def _(pe):
            pe.sem_inc(y_full, N_PROD)
            pe.sem_inc(summed, N_GROUPS)
            pe.sem_inc(mlp_done, MLP)
            pe.wait_ge(consts_made, 3)

            def transpose_field(t, f):
                pe.wait_ge(doubled, before(t, FIELDS) + nth(f) + 1)
                if nth(f) == X_BANKS:
                    pe.wait_ge(xt_copied, FIELDS * t + 1)
                elif not isinstance(t, int) or nth(f) > X_BANKS:
                    pe.wait_ge(x_free, X_USES * t + nth(f) - X_BANKS + (nth(f) < X_BANKS))
                for c in range(ROWSETS):
                    last = nc.tensor.transpose(x_banks[nth(f) % X_BANKS][:, P * c:P * c + P],
                                               twice[:, f % 2, c, :, :].rearrange("p a d -> p (a d)"), ident[:])
                last.then_inc(transposed, 1)

            def multiply_units(t, j):
                y = y_banks[j % Y_SLOTS]
                pe.wait_ge(y_free, before(t, N_PROD) + j - Y_SLOTS + 1)
                for a in range(2):
                    u = 2 * j + a
                    i = UNITS[u][0]
                    if j == first_of_step(i):
                        pe.wait_ge(x_free, freed(t, i))
                    if u == 0 or (2 * u + 1) // RAW_BLOCKS > (2 * u - 1) // RAW_BLOCKS:
                        pe.wait_ge(k_ready, (2 * u + 1) // RAW_BLOCKS + 1)
                    k_unit = k_split[:, 2 * u:2 * u + 2, :].rearrange("p a e -> p (a e)")
                    for x, first in ((x_hi, True), (x_lo, False)):
                        last = nc.tensor.matmul(y[:, a, :], k_unit, x[:, stack_slot(i), :],
                                                start=first, stop=not first)
                last.then_inc(y_full, 1)

            def sum_group(t, g):
                c, s = divmod(g, GROUPS_PER_CHUNK)
                if s == 0:
                    pe.wait_ge(acc_read, before(t, CHUNKS) + c)
                pe.wait_ge(y_free, before(t, N_PROD) + 2 * g + 2)
                for q in range(QUADS):
                    last = nc.tensor.matmul(
                        acc[32 * q:32 * q + 32, :], ones_strip[:, 30 - 2 * s:62 - 2 * s],
                        prod[:, (2 * g + q // 2) % PROD_SLOTS, (q % 2) * TILE:(q % 2 + 1) * TILE],
                        start=s == 0, stop=ends_chunk(g))
                last.then_inc(summed, 1)

            def sum_fields(t):
                pe.wait_ge(x_free, freed(t, 0))
                for s in range(COUPLES // QUADS):
                    for q in range(QUADS):
                        last = nc.tensor.matmul(x_banks[FIELDS % X_BANKS][32 * q:32 * q + 32, :],
                                                ones_strip[:, 30 - 2 * s:62 - 2 * s],
                                                xt[:, QUADS * s + q, :],
                                                start=s == 0, stop=s == COUPLES // QUADS - 1)
                last.then_inc(fields_summed, 1)

            for f in range(FIELDS - 1, FIELDS - 1 - AHEAD, -1):
                transpose_field(0, f)
            with pe.Fori(0, TILES) as t:
                for what in ORDER:
                    if what[0] == "transpose":
                        with guard(pe, t, what[1]):
                            transpose_field(*in_tile(t, what[1]))
                    elif what[0] == "product":
                        multiply_units(t, what[1])
                    elif what[0] == "sum":
                        sum_group(t, what[1])
                    elif what[0] == "fields":
                        sum_fields(t)

            pe.wait_ge(y_free, before(TILES - 1, N_PROD) + N_PROD)
            pe.wait_ge(weights_loaded, 32)
            pe.wait_ge(small_loaded, 48)
            with pe.Fori(0, MLP_PASSES) as i:
                for n, (layer, b, j) in enumerate(MLP_STEPS):
                    if layer == 1 and j == 0:
                        pe.wait_ge(h_loaded[b], 64 * (i + 1))
                    elif layer == 2 and j == 0:
                        pe.wait_ge(mlp_read, before(i, MLP) + mlp_at(1, b, J1 - 1) + 1)
                    elif layer == 3:
                        pe.wait_ge(mlp_read, before(i, MLP) + mlp_at(2, b, J2 - 1) + 1)
                    if n == 7:
                        pe.wait_ge(acc_read, before(TILES - 1, CHUNKS) + CHUNKS)
                    held = n - 8 if n >= 8 else max(x for x in range(MLP) if x % 8 == n) - MLP
                    pe.wait_ge(mlp_read, before(i, MLP) + held + 1)
                    w, x, k = ((w1_sb, h_in, CHUNKS + 1), (w2_sb, h1, J1), (None, h2, J2))[layer - 1]
                    dst = mlp_bank[n % 8] if layer < 3 else mlp_bank[n % 8][0:1, :]
                    for c in range(k):
                        lhs = w3_sb[:, c:c + 1] if layer == 3 else w[:, c, j * P:(j + 1) * P]
                        last = nc.tensor.matmul(dst, lhs, x[b][:, c, :], start=c == 0, stop=c == k - 1)
                    last.then_inc(mlp_done, 1)


def kernel(**inputs):
    import numpy as np
    import concourse.bacc as bacc
    from concourse.bass_utils import run_bass_kernel_spmd

    f32 = mybir.dt.float32
    nc = bacc.Bacc("TRN2", target_bir_lowering=False, num_devices=1)
    arrays = {}

    def dram_in(name, a):
        a = np.ascontiguousarray(a)
        arrays[name] = a
        return nc.dram_tensor(name, a.shape, mybir.dt.from_np(a.dtype), kind="ExternalInput").ap()

    ids = np.asarray(inputs["ids"]).reshape(TILES, ROWSETS, P, FIELDS).transpose(2, 0, 1, 3)
    ids = ids.reshape(P, TILES, ROWSETS * FIELDS)
    index = {}
    for i in range(FIELDS):
        for j in range(i + 1, FIELDS):
            index[(i, j)] = len(index)
    pair_k = np.asarray(inputs["L0_rec_kernels"])
    k = np.zeros((DIM, BLOCKS, DIM), pair_k.dtype)
    w_top1 = np.asarray(inputs["W_top1"])
    w1 = np.zeros((CHUNKS + 1, P, N1), w_top1.dtype)
    for u, (i, m) in enumerate(UNITS):
        c, row = z_row(u)
        for h, f in enumerate(couple_fields(i, m)):
            pair = index[(min(i, f), max(i, f))]
            k[:, 2 * u + h] = pair_k[pair] if i < f else pair_k[pair].T
            w1[c, row + h] = w_top1[FIELDS + pair]
    for f in range(FIELDS):
        w1[CHUNKS, field_row(f)] = w_top1[f]
    w1[CHUNKS, DENSE_ROW:DENSE_ROW + DENSE] = w_top1[FIELDS + PAIRS:]

    args = [
        dram_in("dense_t", np.asarray(inputs["dense_ctx"]).T),
        dram_in("ids", ids),
        [dram_in(f"tbl_{f}", np.asarray(inputs[f"tbl_{f}"])) for f in range(FIELDS)],
        dram_in("pair_k", k.reshape(DIM, BLOCKS * DIM)),
        dram_in("w1", w1.transpose(1, 0, 2)),
        dram_in("b1", np.asarray(inputs["b_top1"]).reshape(J1, P).T),
        dram_in("w2", np.asarray(inputs["W_top2"]).reshape(J1, P, N2).transpose(1, 0, 2)),
        dram_in("b2", np.asarray(inputs["b_top2"]).reshape(J2, P).T),
        dram_in("w3", np.asarray(inputs["W_top3"]).reshape(J2, P).T),
        nc.dram_tensor("sums", (CHUNKS + 1, P, BATCH), f32).ap(),
        nc.dram_tensor("out", (1, BATCH), f32, kind="ExternalOutput").ap(),
    ]
    tower_program(nc, *args)
    r = run_bass_kernel_spmd(nc, [arrays], core_ids=[0])
    return r.results[0]["out"].reshape(BATCH, 1)
```

```python
import concourse.bass as bass
from concourse import mybir
from contextlib import ExitStack, nullcontext

P = 128
BATCH, FIELDS, DIM = 2048, 32, 64
DENSE = 16
N1, N2 = 512, 256
COUPLES = FIELDS // 2
FIELD_QUADS = FIELDS // 4
TILE = 512
TILES = BATCH // TILE
ROWSETS = TILE // P
GATHER_SLOTS = 4
Y_SLOTS = 2
X_BANKS = 3
PROD_SLOTS = 4
QUADS = 4
STACK_SLOTS = 4
UNITS_PER_CHUNK = 64
RAW_CHUNKS = 16
RAW_SLOTS = 4
RAW_PLACE = [3, 2, 1, 0, 3, 2, 1, 0, 2, 1, 0, 2, 1, 0, 1, 0]


def interaction_units():
    units = []
    for quad in range(FIELD_QUADS - 1, -1, -1):
        a, b, c, d = range(4 * quad, 4 * quad + 4)
        above = range(COUPLES - 1, 2 * quad + 1, -1)
        units += [(i, m) for i in (d, c, b) for m in above]
        units += [(b, COUPLES), (c, COUPLES + 1)]
        units += [(a, m) for m in (*above, 2 * quad + 1)]
    for j in range(0, len(units), 2):
        if units[j][1] > units[j + 1][1]:
            units[j], units[j + 1] = units[j + 1], units[j]
    return units


def couple_fields(i, m):
    first = 4 * (i // 4)
    if m == COUPLES:
        return first, first + 3
    if m == COUPLES + 1:
        return first + 1, first + 3
    return 2 * m, 2 * m + 1


UNITS = interaction_units()
PAIRS = FIELDS * (FIELDS - 1) // 2
BLOCKS = 2 * len(UNITS)
CHUNKS = -(-len(UNITS) // UNITS_PER_CHUNK)
RAW_BLOCKS = BLOCKS // RAW_CHUNKS


def last_product(wanted):
    return max(u // 2 for u, unit in enumerate(UNITS) if wanted(*unit))


def last_of_step(i):
    return last_product(lambda a, _: a == i)


def last_of_couple(m):
    return last_product(lambda a, b: b == m or b >= COUPLES and a // 4 == m // 2)


def last_of_quad(quad):
    return last_product(lambda a, b: a // 4 == quad and b >= COUPLES)


def first_of_quad(quad):
    return min(u for u, (a, b) in enumerate(UNITS) if a // 4 == quad and b >= COUPLES) // 2


def last_of_steps(i):
    return max(map(last_of_step, range(i, FIELDS - 1)))


def first_of_step(i):
    return min(u for u, unit in enumerate(UNITS) if unit[0] == i) // 2


def stack_slot(f):
    return STACK_SLOTS - 1 if f == 0 else (FIELDS - 2 - f) % STACK_SLOTS


def slot_before(f):
    g = f + 1
    while g % FIELDS == FIELDS - 1 or stack_slot(g % FIELDS) != stack_slot(f):
        g += 1
    return g if g < FIELDS else g - 2 * FIELDS


N_PROD = len(UNITS) // 2
N_GROUPS = N_PROD // 2
GROUPS_PER_CHUNK = UNITS_PER_CHUNK // QUADS
FIELDS_AT = first_of_step(0)
AHEAD = 6
LEAD = 4
SHORT_STEPS = 7
START = [
    *[("split k", r) for r in range(5)],
    ("double", 31), ("double", 30), ("split k", 5), ("copy", 31), ("copy", 30), ("high", 30),
    ("split k", 6), ("low", 30), ("split k", 7), ("double", 29), ("double", 28), ("split k", 8),
    ("copy", 29), ("high", 29), ("copy", 28), ("high", 28), ("low", 29), ("low", 28),
    ("split k", 9), ("extra", 7), ("split k", 10), ("double", 27), ("double", 26), ("split k", 11),
    ("copy", 27), ("copy", 26), ("split k", 12), ("double", 25), ("double", 24), ("split k", 13)]
RAW_STARTED = sum(what[0] == "split k" for what in START)
assert N_PROD % Y_SLOTS == 0 and N_PROD % PROD_SLOTS == 0 and (FIELDS + 1) % X_BANKS == 0


def plan(first_tile):
    first = FIELDS - 1 - STACK_SLOTS
    transpose_at, high_at = {}, {}
    for f in range(first - 1, -1, -1):
        if f < FIELDS - AHEAD:
            wanted_at = first_of_quad(f // 4) if f % 4 == 0 else first_of_step(f)
            transpose_at[f] = max(last_of_steps(f + 5), transpose_at.get(f + 1, 0),
                                  wanted_at - LEAD if first_tile else 0)
        high_at[f] = max(last_of_steps(slot_before(f)), transpose_at.get(f, 0), high_at.get(f + 1, 0))
    lows, extras = {}, []

    def low_after(j, latest):
        if j < SHORT_STEPS:
            return j
        after = j + 1 + j % 2
        while lows.get(after):
            after += 2
        return max(j, min(after, latest))

    order = [("high", first), ("low", first)]
    group = 0
    for j in range(N_PROD):
        if j == FIELDS_AT:
            order.append(("fields",))
        order.append(("product", j))
        if first_tile and j % 2 == 0 and j // 2 < RAW_CHUNKS - RAW_STARTED:
            order.append(("split k", RAW_STARTED + j // 2))
        if j == FIELDS_AT + 1:
            order.append(("read fields",))
        for f in range(first, -1, -1):
            if transpose_at.get(f) == j:
                for pending in lows.values():
                    if f + X_BANKS in pending:
                        pending.remove(f + X_BANKS)
                        order.append(("low", f + X_BANKS))
                order.append(("transpose", f))
                if f == 4 * (FIELD_QUADS - 2):
                    order.append(("extra", FIELD_QUADS - 2))
            if high_at.get(f) == j:
                order.append(("high", f))
                lows.setdefault(low_after(j, first_of_step(f) - 1), []).append(f)
        for quad in range(FIELD_QUADS - 2):
            if max(last_of_step(4 * quad + 3), transpose_at[4 * quad]) == j:
                extras.append(("extra", quad))
        order += [("low", f) for f in lows.pop(j, ())]
        if j % 2 == 1 and j >= 3:
            order.append(("sum", group))
            group += 1
            order += extras
            extras = []
        for n, step in enumerate((1, 2, 3, 4, 6)):
            if j == FIELDS_AT + step:
                f = 2 * FIELDS - 1 - n
                order.append(("transpose", f))
                if 1 <= n < STACK_SLOTS:
                    order.append(("high", f))
                    lows.setdefault(low_after(j, N_PROD - 1), []).append(f)
                if n == 3:
                    order.append(("extra", 2 * FIELD_QUADS - 1))
    order.append(("transpose", 2 * FIELDS - AHEAD))
    order.append(("sum", group))
    assert not lows
    return order


FIRST_ORDER, ORDER = plan(True), plan(False)


def z_row(u):
    c, r = divmod(u, UNITS_PER_CHUNK)
    s, q = divmod(r, QUADS)
    return c, 32 * q + 2 * s


def field_row(f):
    s, q = divmod(f // 2, QUADS)
    return SUM_ROWS * q + 2 * s + f % 2


def ends_chunk(g):
    return g % GROUPS_PER_CHUNK == GROUPS_PER_CHUNK - 1 or g == N_GROUPS - 1


DENSE_ROW = 2 * (N_GROUPS % GROUPS_PER_CHUNK)
DENSE_ROWS = DENSE // QUADS
SUM_ROWS = 2 * (COUPLES // QUADS)
assert DENSE_ROW + DENSE_ROWS == 32 and QUADS * SUM_ROWS == 32

EVACS = [*range(CHUNKS - 1), CHUNKS, CHUNKS - 1]
N_EVACS = len(EVACS)
J1, J2 = N1 // P, N2 // P
MLP_STEPS = [(layer, b, j) for layer, n in ((1, J1), (2, J2), (3, 1)) for b in range(2) for j in range(n)]
MLP = len(MLP_STEPS)
MLP_PASSES = TILES // 2


def mlp_at(layer, b, j):
    return MLP_STEPS.index((layer, b, j))


def tower_program(nc, dense_t, ids, tables, pair_k, w1, b1, w2, b2, w3, sums, out):
    f32, f32r, i32 = mybir.dt.float32, mybir.dt.float32r, mybir.dt.int32
    ACT = mybir.ActivationFunctionType
    ALU = mybir.AluOpType

    with ExitStack() as ctx:
        def sb(name, shape, dt):
            return ctx.enter_context(nc.sbuf_tensor(name, shape, dt))

        def bank(name, shape):
            return ctx.enter_context(nc.psum_tensor(name, shape, f32))

        def sem(name):
            return ctx.enter_context(nc.semaphore(name))

        k_split = sb("k_split", [P, BLOCKS, DIM], f32r)
        x_hi = sb("x_hi", [P, STACK_SLOTS, TILE], f32r)
        x_lo = sb("x_lo", [P, STACK_SLOTS, TILE], f32r)
        xt = sb("xt", [P, COUPLES + 2, TILE], f32)
        prod = sb("prod", [P, PROD_SLOTS, 2 * TILE], f32)
        rows = sb("rows", [P, GATHER_SLOTS, ROWSETS, 2, DIM], f32)
        twice = sb("twice", [P, 2, ROWSETS, 2, DIM], f32)
        sums_sb = sb("sums_sb", [P, TILE], f32)
        ids_now = sb("ids_now", [P, ROWSETS * FIELDS], i32)
        ones_strip = sb("ones_strip", [P, 62], f32)
        ident = sb("ident", [P, P], f32)
        b1_sb = sb("b1_sb", [P, J1], f32)
        b2_sb = sb("b2_sb", [P, J2], f32)
        w3_sb = sb("w3_sb", [P, J2], f32)

        xt_flat = xt[:, :, :].rearrange("p m b -> p (m b)")
        raw_cols = RAW_BLOCKS * DIM
        raw = [xt_flat[0:DIM, r * raw_cols:(r + 1) * raw_cols].rearrange("p (k e) -> p k e", e=DIM)
               for r in range(RAW_SLOTS)]
        prod_flat = prod[:, :, :].rearrange("p s b -> p (s b)").rearrange("p (s b) -> p s b", b=TILE)
        rows_flat = rows[:, :, :, :, :].rearrange("p s c h d -> p (s c h d)").rearrange(
            "p (s b) -> p s b", b=TILE)
        w1_sb = xt[:, COUPLES - CHUNKS - 1:COUPLES, :]
        w2_sb = twice[:, :, :, :, :].rearrange("p h c a d -> p (h c a d)").rearrange("p (k n) -> p k n", k=J1)
        h_in_first = COUPLES - 2 * (CHUNKS + 1)
        h_in = [xt[:, h_in_first:h_in_first + CHUNKS + 1, :], prod_flat[:, 0:CHUNKS + 1, :]]
        h1 = [xt[:, J2:J2 + J1, :], rows_flat]
        h2 = [xt[:, 0:J2, :], prod_flat[:, CHUNKS + 1:CHUNKS + 1 + J2, :]]
        y_sb = [prod_flat[0:1, CHUNKS + 1 + J2, :], sums_sb[0:1, :]]

        k_flat = k_split[:, :, :].rearrange("p k e -> p (k e)")
        w_parts = k_flat[:, 0:N1]
        z_parts = [k_flat[:, N1 + TILE * b:N1 + TILE * (b + 1)] for b in range(2)]

        y_banks = [bank(f"y{i}", [P, 2, TILE]) for i in range(Y_SLOTS)]
        acc = bank("acc", [P, TILE])
        x_banks = [bank(f"x{i}", [P, TILE]) for i in range(X_BANKS)]
        mlp_bank = [y_banks[b // 2][:, b % 2, :] for b in range(2 * Y_SLOTS)] + \
            [x[:] for x in x_banks] + [acc[:]]

        ids_loaded = sem("ids_loaded")
        ident_zeroed = sem("ident_zeroed")
        strip_zeroed = sem("strip_zeroed")
        consts_made = sem("consts_made")
        raw_loaded = [sem(f"raw_loaded{r}") for r in range(RAW_SLOTS)]
        k_high = sem("k_high")
        k_ready = sem("k_ready")
        pool_passed = sem("pool_passed")
        act_passed = sem("act_passed")
        gathered = [sem(f"gathered{s}") for s in range(GATHER_SLOTS)]
        doubled = sem("doubled")
        transposed = sem("transposed")
        xt_copied = sem("xt_copied")
        high_made = sem("high_made")
        extra_made = sem("extra_made")
        x_free = sem("x_free")
        y_full = sem("y_full")
        y_free = sem("y_free")
        summed = sem("summed")
        fields_summed = sem("fields_summed")
        acc_read = sem("acc_read")
        stored = sem("stored")
        small_loaded = sem("small_loaded")
        weights_loaded = sem("weights_loaded")
        h_loaded = [sem(f"h_loaded{b}") for b in range(2)]
        z_loaded = [sem(f"z_loaded{b}") for b in range(2)]
        w_high = sem("w_high")
        w_split = sem("w_split")
        z_high = sem("z_high")
        z_split = sem("z_split")
        mlp_done = sem("mlp_done")
        mlp_read = sem("mlp_read")
        out_stored = [sem(f"out_stored{b}") for b in range(2)]

        block = ctx.enter_context(nc.Block())

        def before(t, n):
            return (t + 1) * n

        ROWS_IN = COUPLES // GATHER_SLOTS * ROWSETS * 2 * 16

        def raw_slot(r):
            return RAW_PLACE[r], RAW_PLACE[:r].count(RAW_PLACE[r])

        def left(slot):
            return max(r for r in range(RAW_CHUNKS) if RAW_PLACE[r] == slot) + 1

        H_LOADS = 16 * (1 + 2 * QUADS)
        Z_LOADS = 16 * QUADS

        def nth(f):
            return FIELDS - 1 - f

        X_USES = FIELDS

        def freed(t, f):
            return X_USES * t + nth(f)

        def in_tile(t, f):
            return (t, f) if f < FIELDS else (t + 1, f - FIELDS)

        def guard(engine, t, f):
            return engine.If(t < TILES - 1) if f >= FIELDS and not isinstance(t, int) else nullcontext()

        @block.gpsimd
        def _(pool):
            pool.memset(ident[:], 0.0).then_inc(ident_zeroed, 1)
            pool.wait_ge(ident_zeroed, 1)
            pool.affine_select(out=ident[:], in_=ident[:], compare_op=ALU.not_equal, fill=1.0, base=0,
                               pattern=[[-1, P]], channel_multiplier=1).then_inc(consts_made, 1)
            with pool.Fori(0, TILES) as t:
                pool.dma_start(ids_now[:], ids[:, bass.ds(t, 1), :].rearrange("p o n -> p (o n)")
                               ).then_inc(ids_loaded, 16)
                pool.wait_ge(ids_loaded, 16 * (t + 1))
                pool.sem_inc(pool_passed, 1)
                for k in range(COUPLES):
                    m, s = COUPLES - 1 - k, k % GATHER_SLOTS
                    pool.wait_ge(doubled, before(t, FIELDS) + 2 * (k - GATHER_SLOTS) + 2)
                    pool.sem_inc(pool_passed, 1)
                    for h in (1, 0):
                        for c in range(ROWSETS):
                            f = 2 * m + h
                            pool.indirect_dma_start(
                                out=rows[:, s, c, h, :], out_offset=None, in_=tables[f],
                                in_offset=bass.IndirectOffsetOnAxis(
                                    ap=ids_now[:, c * FIELDS + f:c * FIELDS + f + 1], axis=0)
                            ).then_inc(gathered[s], 16)
                for s in range(GATHER_SLOTS):
                    pool.wait_ge(gathered[s], before(t, ROWS_IN))
                    pool.sem_inc(pool_passed, 1)

        @block.sync
        def _(sp):
            for r in range(RAW_CHUNKS):
                s, used = raw_slot(r)
                if used:
                    sp.wait_ge(k_ready, max(q for q in range(r) if raw_slot(q)[0] == s) + 1)
                sp.dma_start(raw[s],
                             pair_k[:, r * raw_cols:(r + 1) * raw_cols].rearrange("p (k e) -> p k e", e=DIM)
                             ).then_inc(raw_loaded[s], 16)
            sp.dma_start(b1_sb[:], b1).then_inc(small_loaded, 16)
            sp.dma_start(b2_sb[:], b2).then_inc(small_loaded, 16)
            sp.dma_start(w3_sb[:], w3).then_inc(small_loaded, 16)

            def store_sums(t, n):
                if EVACS[n] == CHUNKS:
                    sp.wait_ge(x_free, X_USES * (t + 1))
                else:
                    sp.wait_ge(acc_read, before(t, CHUNKS) + EVACS[n] + 1)
                sp.dma_start(sums[EVACS[n], :, bass.ds(t * TILE, TILE)], sums_sb[:]).then_inc(stored, 16)

            with sp.Fori(0, TILES - 1) as t:
                for n in range(N_EVACS):
                    store_sums(t, n)
            t = TILES - 1
            for n in range(N_EVACS - 1):
                store_sums(t, n)
            sp.wait_ge(transposed, TILES * FIELDS)
            sp.dma_start(w2_sb, w2).then_inc(weights_loaded, 16)
            sp.wait_ge(y_free, before(t, N_PROD) + last_of_couple(COUPLES - CHUNKS - 1) + 1)
            sp.dma_start(w1_sb, w1).then_inc(weights_loaded, 16)

            def load_h(n, b):
                cols = bass.ds(n * TILE, TILE)
                sp.dma_start(h_in[b][:, 0:CHUNKS - 1, :], sums[0:CHUNKS - 1, :, cols].rearrange("c p b -> p c b")
                             ).then_inc(h_loaded[b], 16)
                for q in range(QUADS):
                    lo, mid, hi = 32 * q, 32 * q + DENSE_ROW, 32 * q + 32
                    sp.dma_start(h_in[b][lo:mid, CHUNKS - 1, :], sums[CHUNKS - 1, lo:mid, cols]
                                 ).then_inc(h_loaded[b], 16)
                    sp.dma_start(h_in[b][mid:hi, CHUNKS - 1, :],
                                 dense_t[DENSE_ROWS * q:DENSE_ROWS * (q + 1), cols]).then_inc(h_loaded[b], 16)
                for part in range(QUADS):
                    sp.dma_start(h_in[b][32 * part:32 * part + 32, CHUNKS, :],
                                 sums[CHUNKS, :, cols].rearrange("(q r) b -> q r b", q=QUADS)[:, 0:SUM_ROWS, :]
                                 ).then_inc(z_loaded[b], 16)

            sp.wait_ge(y_free, before(t, N_PROD) + last_of_couple(h_in_first) + 1)
            sp.wait_ge(stored, 16 * (N_EVACS + 1))
            load_h(0, 0)
            store_sums(t, N_EVACS - 1)
            sp.wait_ge(summed, before(t, N_GROUPS) + N_GROUPS)
            sp.wait_ge(stored, 16 * (TILES * N_EVACS + 1))
            load_h(1, 1)
            with sp.Fori(1, MLP_PASSES) as i:
                for b in range(2):
                    sp.wait_ge(mlp_done, i * MLP + mlp_at(1, b, J1 - 1) + 1)
                    load_h(2 * i + b, b)

        @block.scalar
        def _(act):
            act.sem_inc(acc_read, CHUNKS)
            act.sem_inc(stored, 16)
            act.sem_inc(doubled, FIELDS)
            act.sem_inc(mlp_read, MLP)
            for b in range(2):
                act.sem_inc(out_stored[b], 16)

            def double(t, f):
                k, s = nth(f) // 2, nth(f) // 2 % GATHER_SLOTS
                act.wait_ge(gathered[s], ROWS_IN * t + (k // GATHER_SLOTS + 1) * (ROWSETS * 32))
                nc.scalar.copy(twice[:, f % 2, :, :, :],
                               rows[:, s, :, f % 2:f % 2 + 1, :].to_broadcast([P, ROWSETS, 2, DIM])
                               ).then_inc(doubled, 1)

            def copy_field(t, f):
                act.wait_ge(transposed, FIELDS * t + nth(f) + 1)
                act.wait_ge(y_free, before(t, N_PROD) - N_PROD + last_of_couple(f // 2) + 1)
                part = slice(DIM * (f % 2), DIM * (f % 2) + DIM)
                nc.scalar.copy(xt[part, f // 2, :], x_banks[nth(f) % X_BANKS][part, :]).then_inc(xt_copied, 1)

            def make_high(t, f):
                g = slot_before(f)
                act.wait_ge(y_full, before(t, N_PROD) + (last_of_step(g) if g >= 0 else
                                                         last_of_step(g + FIELDS) - N_PROD) + 1)
                nc.scalar.copy(x_hi[:, stack_slot(f), :], x_banks[nth(f) % X_BANKS][:]
                               ).then_inc(high_made, 1)

            def make_extra(t, quad):
                last = last_of_quad(quad + 1) if quad < FIELD_QUADS - 1 else last_of_quad(0) - N_PROD
                act.wait_ge(y_free, before(t, N_PROD) + last + 1)
                act.wait_ge(xt_copied, FIELDS * t + nth(4 * quad) + 1)
                nc.scalar.copy(xt[0:DIM, COUPLES, :], xt[0:DIM, 2 * quad, :]).then_inc(extra_made, 1)
                nc.scalar.copy(xt[0:DIM, COUPLES + 1, :], xt[DIM:P, 2 * quad, :]).then_inc(extra_made, 1)
                nc.scalar.copy(xt[DIM:P, COUPLES:COUPLES + 2, :],
                               xt[DIM:P, 2 * quad + 1:2 * quad + 2, :].to_broadcast([DIM, 2, TILE])
                               ).then_inc(extra_made, 1)

            def k_high_part(r):
                s, used = raw_slot(r)
                act.wait_ge(raw_loaded[s], 16 * (used + 1))
                nc.scalar.copy(k_split[0:DIM, r * RAW_BLOCKS:(r + 1) * RAW_BLOCKS, :], raw[s]
                               ).then_inc(k_high, 1)

            for what, n in START:
                if what == "split k":
                    k_high_part(n)
                elif what == "double":
                    double(0, n)
                elif what == "copy":
                    if n == FIELDS - 1:
                        act.wait_ge(k_ready, left(3))
                    copy_field(0, n)
                elif what == "high":
                    make_high(0, n)
                elif what == "extra":
                    make_extra(0, n)
            act.wait_ge(k_ready, left(2))
            def tile(t, order):
                for what in order:
                    if what[0] == "transpose":
                        f = what[1]
                        with guard(act, t, f):
                            copy_field(*in_tile(t, f))
                        with guard(act, t, f if f >= 2 else FIELDS):
                            double(*in_tile(t, f - 2 if f >= 2 else f - 2 + 2 * FIELDS))
                    elif what[0] == "split k":
                        k_high_part(what[1])
                        if what[1] == RAW_CHUNKS - 1:
                            act.wait_ge(k_ready, RAW_CHUNKS)
                            act.sem_inc(act_passed, 1)
                    elif what[0] == "extra":
                        with guard(act, t, 4 * what[1]):
                            make_extra(*((t, what[1]) if what[1] < FIELD_QUADS else
                                         (t + 1, what[1] - FIELD_QUADS)))
                    elif what[0] == "high":
                        with guard(act, t, what[1]):
                            make_high(*in_tile(t, what[1]))
                    elif what[0] == "sum" and ends_chunk(what[1]):
                        act.wait_ge(summed, before(t, N_GROUPS) + what[1] + 1)
                        n = EVACS.index(what[1] // GROUPS_PER_CHUNK)
                        act.wait_ge(stored, 16 * (t * N_EVACS + n + 1))
                        nc.scalar.copy(sums_sb[:], acc[:]).then_inc(acc_read, 1)

            tile(0, FIRST_ORDER)
            with act.Fori(1, TILES) as t:
                tile(t, ORDER)
            act.wait_ge(y_free, before(TILES - 1, N_PROD) + N_PROD)
            act.wait_ge(summed, before(TILES - 1, N_GROUPS) + N_GROUPS)
            act.wait_ge(stored, 16 * (TILES * N_EVACS + 1))
            act.wait_ge(small_loaded, 48)
            with act.Fori(0, MLP_PASSES) as i:
                for n, (layer, b, j) in enumerate(MLP_STEPS):
                    act.wait_ge(mlp_done, before(i, MLP) + n + 1)
                    src = mlp_bank[n % 8]
                    if layer == 1:
                        nc.scalar.activation(h1[b][:, j, :], src, ACT.Relu, bias=b1_sb[:, j:j + 1]
                                             ).then_inc(mlp_read, 1)
                    elif layer == 2:
                        nc.scalar.activation(h2[b][:, j, :], src, ACT.Relu, bias=b2_sb[:, j:j + 1]
                                             ).then_inc(mlp_read, 1)
                    else:
                        act.wait_ge(out_stored[b], 16 * (i + 1))
                        nc.scalar.copy(y_sb[b], src[0:1, :]).then_inc(mlp_read, 1)
                        act.wait_ge(mlp_read, before(i, MLP) + n + 1)
                        act.dma_start(out[0:1, bass.ds((2 * i + b) * TILE, TILE)], y_sb[b]
                                      ).then_inc(out_stored[b], 16)
            for b in range(2):
                act.wait_ge(out_stored[b], 16 * (MLP_PASSES + 1))

        @block.vector
        def _(dve):
            dve.memset(ones_strip[:], 0.0).then_inc(strip_zeroed, 1)
            dve.wait_ge(strip_zeroed, 1)
            dve.memset(ones_strip[0:DIM, 30:31], 1.0).then_inc(consts_made, 1)
            dve.memset(ones_strip[DIM:P, 31:32], 1.0).then_inc(consts_made, 1)
            dve.sem_inc(y_free, N_PROD)

            def k_low_part(r):
                blocks = slice(r * RAW_BLOCKS, (r + 1) * RAW_BLOCKS)
                dve.wait_ge(k_high, r + 1)
                nc.vector.tensor_tensor(k_split[DIM:P, blocks, :], raw[raw_slot(r)[0]],
                                        k_split[0:DIM, blocks, :], ALU.subtract).then_inc(k_ready, 1)

            def make_low(t, f):
                x = x_banks[nth(f) % X_BANKS]
                dve.wait_ge(xt_copied, FIELDS * t + nth(f) + 1)
                dve.wait_ge(high_made, (FIELDS - 1) * t + nth(f))
                nc.vector.tensor_tensor(x_lo[:, stack_slot(f), :], x[:], x_hi[:, stack_slot(f), :],
                                        ALU.subtract).then_inc(x_free, 1)

            def multiply(t, j):
                dve.wait_ge(y_full, before(t, N_PROD) + j + 1)
                dve.wait_ge(summed, before(t, N_GROUPS) + (j - PROD_SLOTS) // 2 + 1)
                for a, m in UNITS[2 * j:2 * j + 2]:
                    if m >= COUPLES:
                        dve.wait_ge(extra_made, 3 * (FIELD_QUADS * t + FIELD_QUADS - a // 4))
                m0, m1 = UNITS[2 * j][1], UNITS[2 * j + 1][1]
                x = xt[:, m0:m1 + 1:m1 - m0, :] if m1 > m0 else xt[:, m0:m0 + 1, :].to_broadcast([P, 2, TILE])
                nc.vector.tensor_tensor(prod[:, j % PROD_SLOTS, :].rearrange("p (a b) -> p a b", a=2),
                                        y_banks[j % Y_SLOTS][:, :, :], x, ALU.mult).then_inc(y_free, 1)

            def read_fields(t):
                dve.wait_ge(fields_summed, t + 1)
                dve.wait_ge(stored, 16 * (t * N_EVACS + CHUNKS))
                nc.vector.tensor_copy(sums_sb[:], x_banks[FIELDS % X_BANKS][:]).then_inc(x_free, 1)

            for what, n in START:
                if what == "split k":
                    k_low_part(n)
                elif what == "low":
                    make_low(0, n)
            def tile(t, order):
                for what in order:
                    if what[0] == "product":
                        multiply(t, what[1])
                    elif what[0] == "read fields":
                        read_fields(t)
                    elif what[0] == "split k":
                        k_low_part(what[1])
                    elif what[0] == "low":
                        with guard(dve, t, what[1]):
                            make_low(*in_tile(t, what[1]))

            tile(0, FIRST_ORDER)
            with dve.Fori(1, TILES) as t:
                tile(t, ORDER)
            dve.wait_ge(y_full, before(TILES - 1, N_PROD) + N_PROD)
            dve.wait_ge(weights_loaded, 32)
            nc.vector.tensor_copy(w_parts, w1_sb[:, CHUNKS, :]).then_inc(w_high, 1)
            dve.wait_ge(w_high, 1)
            nc.vector.tensor_tensor(w_parts[DIM:P, :], w1_sb[DIM:P, CHUNKS, :], w_parts[DIM:P, :],
                                    ALU.subtract).then_inc(w_split, 1)
            with dve.Fori(0, MLP_PASSES) as i:
                for b in range(2):
                    dve.wait_ge(z_loaded[b], Z_LOADS * (i + 1))
                    dve.wait_ge(mlp_done, before(i, MLP) - MLP + mlp_at(1, b, J1 - 1) + 1)
                    nc.vector.tensor_copy(z_parts[b], h_in[b][:, CHUNKS, :]).then_inc(z_high, 1)
                    dve.wait_ge(z_high, 2 * i + b + 1)
                    for lo in (32, 96):
                        nc.vector.tensor_tensor(z_parts[b][lo:lo + 32, :], h_in[b][lo:lo + 32, CHUNKS, :],
                                                z_parts[b][lo:lo + 32, :], ALU.subtract).then_inc(z_split, 1)

        @block.tensor
        def _(pe):
            pe.sem_inc(y_full, N_PROD)
            pe.sem_inc(summed, N_GROUPS)
            pe.sem_inc(mlp_done, MLP)
            pe.wait_ge(consts_made, 3)

            def transpose_field(t, f):
                pe.wait_ge(doubled, before(t, FIELDS) + nth(f) + 1)
                if nth(f) == X_BANKS:
                    pe.wait_ge(xt_copied, FIELDS * t + 1)
                elif not isinstance(t, int) or t > 0 or nth(f) > X_BANKS:
                    pe.wait_ge(x_free, X_USES * t + nth(f) - X_BANKS + (nth(f) < X_BANKS))
                for c in range(ROWSETS):
                    last = nc.tensor.transpose(x_banks[nth(f) % X_BANKS][:, P * c:P * c + P],
                                               twice[:, f % 2, c, :, :].rearrange("p a d -> p (a d)"), ident[:])
                last.then_inc(transposed, 1)

            def multiply_units(t, j):
                y = y_banks[j % Y_SLOTS]
                pe.wait_ge(y_free, before(t, N_PROD) + j - Y_SLOTS + 1)
                for a in range(2):
                    u = 2 * j + a
                    i = UNITS[u][0]
                    if j == first_of_step(i):
                        pe.wait_ge(x_free, freed(t, i))
                    if u == 0 or (2 * u + 1) // RAW_BLOCKS > (2 * u - 1) // RAW_BLOCKS:
                        pe.wait_ge(k_ready, (2 * u + 1) // RAW_BLOCKS + 1)
                    k_unit = k_split[:, 2 * u:2 * u + 2, :].rearrange("p a e -> p (a e)")
                    for x, first in ((x_hi, True), (x_lo, False)):
                        last = nc.tensor.matmul(y[:, a, :], k_unit, x[:, stack_slot(i), :],
                                                start=first, stop=not first)
                last.then_inc(y_full, 1)

            def sum_group(t, g):
                c, s = divmod(g, GROUPS_PER_CHUNK)
                if s == 0:
                    pe.wait_ge(acc_read, before(t, CHUNKS) + c)
                pe.wait_ge(y_free, before(t, N_PROD) + 2 * g + 2)
                for q in range(QUADS):
                    last = nc.tensor.matmul(
                        acc[32 * q:32 * q + 32, :], ones_strip[:, 30 - 2 * s:62 - 2 * s],
                        prod[:, (2 * g + q // 2) % PROD_SLOTS, (q % 2) * TILE:(q % 2 + 1) * TILE],
                        start=s == 0, stop=ends_chunk(g))
                last.then_inc(summed, 1)

            def sum_fields(t):
                pe.wait_ge(x_free, freed(t, 0))
                for s in range(COUPLES // QUADS):
                    for q in range(QUADS):
                        last = nc.tensor.matmul(x_banks[FIELDS % X_BANKS][32 * q:32 * q + 32, :],
                                                ones_strip[:, 30 - 2 * s:62 - 2 * s],
                                                xt[:, QUADS * s + q, :],
                                                start=s == 0, stop=s == COUPLES // QUADS - 1)
                last.then_inc(fields_summed, 1)

            for f in range(FIELDS - 1, FIELDS - 1 - AHEAD, -1):
                transpose_field(0, f)
            def tile(t, order):
                for what in order:
                    if what[0] == "transpose":
                        with guard(pe, t, what[1]):
                            transpose_field(*in_tile(t, what[1]))
                    elif what[0] == "product":
                        multiply_units(t, what[1])
                    elif what[0] == "sum":
                        sum_group(t, what[1])
                    elif what[0] == "fields":
                        sum_fields(t)

            tile(0, FIRST_ORDER)
            with pe.Fori(1, TILES) as t:
                tile(t, ORDER)

            pe.wait_ge(y_free, before(TILES - 1, N_PROD) + N_PROD)
            pe.wait_ge(weights_loaded, 32)
            pe.wait_ge(small_loaded, 48)
            with pe.Fori(0, MLP_PASSES) as i:
                for n, (layer, b, j) in enumerate(MLP_STEPS):
                    if layer == 1 and j == 0:
                        pe.wait_ge(h_loaded[b], H_LOADS * (i + 1))
                    elif layer == 2 and j == 0:
                        pe.wait_ge(mlp_read, before(i, MLP) + mlp_at(1, b, J1 - 1) + 1)
                    elif layer == 3:
                        pe.wait_ge(mlp_read, before(i, MLP) + mlp_at(2, b, J2 - 1) + 1)
                    if n == 7:
                        pe.wait_ge(acc_read, before(TILES - 1, CHUNKS) + CHUNKS)
                    held = n - 8 if n >= 8 else max(x for x in range(MLP) if x % 8 == n) - MLP
                    pe.wait_ge(mlp_read, before(i, MLP) + held + 1)
                    w, x, k = ((w1_sb, h_in, CHUNKS + 1), (w2_sb, h1, J1), (None, h2, J2))[layer - 1]
                    dst = mlp_bank[n % 8] if layer < 3 else mlp_bank[n % 8][0:1, :]
                    for c in range(k):
                        if layer == 1 and c == CHUNKS:
                            pe.wait_ge(w_split, 1)
                            pe.wait_ge(z_split, 4 * i + 2 * b + 2)
                            last = nc.tensor.matmul(dst, w_parts[:, j * P:(j + 1) * P], z_parts[b],
                                                    start=False, stop=True)
                            continue
                        lhs = w3_sb[:, c:c + 1] if layer == 3 else w[:, c, j * P:(j + 1) * P]
                        last = nc.tensor.matmul(dst, lhs, x[b][:, c, :], start=c == 0, stop=c == k - 1)
                    last.then_inc(mlp_done, 1)


def kernel(**inputs):
    import numpy as np
    import concourse.bacc as bacc
    from concourse.bass_utils import run_bass_kernel_spmd

    f32 = mybir.dt.float32
    nc = bacc.Bacc("TRN2", target_bir_lowering=False, num_devices=1)
    arrays = {}

    def dram_in(name, a):
        a = np.ascontiguousarray(a)
        arrays[name] = a
        return nc.dram_tensor(name, a.shape, mybir.dt.from_np(a.dtype), kind="ExternalInput").ap()

    ids = np.asarray(inputs["ids"]).reshape(TILES, ROWSETS, P, FIELDS).transpose(2, 0, 1, 3)
    ids = ids.reshape(P, TILES, ROWSETS * FIELDS)
    index = {}
    for i in range(FIELDS):
        for j in range(i + 1, FIELDS):
            index[(i, j)] = len(index)
    pair_k = np.asarray(inputs["L0_rec_kernels"])
    k = np.zeros((DIM, BLOCKS, DIM), pair_k.dtype)
    w_top1 = np.asarray(inputs["W_top1"])
    w1 = np.zeros((CHUNKS + 1, P, N1), w_top1.dtype)
    for u, (i, m) in enumerate(UNITS):
        c, row = z_row(u)
        for h, f in enumerate(couple_fields(i, m)):
            pair = index[(min(i, f), max(i, f))]
            k[:, 2 * u + h] = pair_k[pair] if i < f else pair_k[pair].T
            w1[c, row + h] = w_top1[FIELDS + pair]
    for part in range(QUADS):
        for f in range(FIELDS):
            w1[CHUNKS, 32 * part + field_row(f)] = w_top1[f]
        w1[CHUNKS - 1, 32 * part + DENSE_ROW:32 * part + 32] = \
            w_top1[FIELDS + PAIRS + DENSE_ROWS * part:FIELDS + PAIRS + DENSE_ROWS * (part + 1)]

    args = [
        dram_in("dense_t", np.asarray(inputs["dense_ctx"]).T),
        dram_in("ids", ids),
        [dram_in(f"tbl_{f}", np.asarray(inputs[f"tbl_{f}"])) for f in range(FIELDS)],
        dram_in("pair_k", k.reshape(DIM, BLOCKS * DIM)),
        dram_in("w1", w1.transpose(1, 0, 2)),
        dram_in("b1", np.asarray(inputs["b_top1"]).reshape(J1, P).T),
        dram_in("w2", np.asarray(inputs["W_top2"]).reshape(J1, P, N2).transpose(1, 0, 2)),
        dram_in("b2", np.asarray(inputs["b_top2"]).reshape(J2, P).T),
        dram_in("w3", np.asarray(inputs["W_top3"]).reshape(J2, P).T),
        nc.dram_tensor("sums", (CHUNKS + 1, P, BATCH), f32).ap(),
        nc.dram_tensor("out", (1, BATCH), f32, kind="ExternalOutput").ap(),
    ]
    tower_program(nc, *args)
    r = run_bass_kernel_spmd(nc, [arrays], core_ids=[0])
    return r.results[0]["out"].reshape(BATCH, 1)
```
